# Optimizing a Trainium2 kernel written in Bass

```python
import numpy as np
import jax
import jax.numpy as jnp

def _softmax(x, axis=-1):
    return jax.nn.softmax(x, axis=axis)

def _gelu(x):
    return jax.nn.gelu(x, approximate=True)

def _silu(x):
    return jax.nn.silu(x)

def _sigmoid(x):
    return jax.nn.sigmoid(x)

def _layernorm(x, axis=-1, eps=1e-05):
    m = jnp.mean(x, axis=axis, keepdims=True)
    v = jnp.var(x, axis=axis, keepdims=True)
    return (x - m) / jnp.sqrt(v + eps)

def _scatter_add(tgt, idx, src, axis=0):
    return tgt.at[idx].add(src)

def _segment_sum(src, seg, n):
    return jax.ops.segment_sum(src, seg, n)
kernel_name = 'mk_adaln_ffn_d1_seqx_r4_98a29b'

def setup_inputs(seed: int=0):
    np.random.seed(seed)
    _w = jnp.asarray

    def _rec_inputs():
        import jax
        import jax.numpy as jnp
        _rk = jax.random.key(seed)
        x = -0.0003929 + 0.9999 * jax.random.normal(jax.random.fold_in(_rk, 1), (8, 256, 512), jnp.float32)
        _lenS = 256 - jax.random.randint(jax.random.fold_in(_rk, 7), (8,), 0, max(1, 256 // 4) + 1, jnp.int32)
        _lenS2 = 256 - jax.random.randint(jax.random.fold_in(_rk, 8), (8,), 0, max(1, 256 // 4) + 1, jnp.int32)
        cond_2048 = 0.00782532 + 1.00527 * jax.random.normal(jax.random.fold_in(_rk, 11), (8, 512), jnp.float32)
        return (x, cond_2048)
    x, cond_2048 = _rec_inputs()

    def _L0_cond_setup():
        import jax, jax.numpy as jnp
        import numpy as np
        HEADS = 16
        EPS = 1e-06

        def _rms_norm(x, g):
            xf = x.astype(jnp.float32)
            y = xf * jax.lax.rsqrt(jnp.mean(xf * xf, axis=-1, keepdims=True) + EPS)
            return y.astype(x.dtype) * g
        key = jax.random.key(seed)
        ks = jax.random.split(key, 6)
        b, n, dim, emb_dim = (4, 512, 512, 512)
        d_head = dim // HEADS
        return {'x': jax.random.normal(ks[0], (b, n, dim), jnp.float32), 'emb': jax.random.normal(ks[1], (b, 1, emb_dim), jnp.float32), 'W_emb': jax.random.normal(ks[2], (emb_dim, 2 * dim), jnp.float32) * emb_dim ** (-0.5), 'b_emb': jnp.zeros((2 * dim,), jnp.float32), 'g_norm': jnp.ones((dim,), jnp.float32), 'W_qkv': jax.random.normal(ks[3], (dim, 3 * dim), jnp.float32) * dim ** (-0.5), 'g_q': jnp.ones((d_head,), jnp.float32), 'g_k': jnp.ones((d_head,), jnp.float32), 'W_out': jax.random.normal(ks[4], (dim, dim), jnp.float32) * dim ** (-0.5)}
    _L0_cond_all = _L0_cond_setup()
    _L0_cond_in = {k: v for k, v in _L0_cond_all.items() if k in ('W_emb', 'b_emb', 'g_norm', 'W_qkv', 'g_q', 'g_k', 'W_out')}
    del _L0_cond_all

    def _L0_ffn_setup():
        import jax, jax.numpy as jnp
        import numpy as np
        TOP_K = 2
        key = jax.random.key(seed)
        k1, k2, k3, k4, k5 = jax.random.split(key, 5)
        B, S, D = (2, 512, 512)
        E, H = (8, 256)
        scale_in = 1.0 / np.sqrt(D)
        scale_h = 1.0 / np.sqrt(H)
        return {'hidden_states': jax.random.normal(k1, (B, S, D), dtype=jnp.float32), 'W_gate': jax.random.normal(k2, (E, D), dtype=jnp.float32) * scale_in, 'w_gate_proj': jax.random.normal(k3, (E, D, H), dtype=jnp.float32) * scale_in, 'w_up_proj': jax.random.normal(k4, (E, D, H), dtype=jnp.float32) * scale_in, 'w_down_proj': jax.random.normal(k5, (E, H, D), dtype=jnp.float32) * scale_h}
    _L0_ffn_all = _L0_ffn_setup()
    _L0_ffn_in = {k: v for k, v in _L0_ffn_all.items() if k in ('W_gate', 'w_gate_proj', 'w_up_proj', 'w_down_proj')}
    del _L0_ffn_all
    return {'x': x, 'cond_2048': cond_2048, 'L0_cond_W_emb': _L0_cond_in['W_emb'], 'L0_cond_b_emb': _L0_cond_in['b_emb'], 'L0_cond_g_norm': _L0_cond_in['g_norm'], 'L0_cond_W_qkv': _L0_cond_in['W_qkv'], 'L0_cond_g_q': _L0_cond_in['g_q'], 'L0_cond_g_k': _L0_cond_in['g_k'], 'L0_cond_W_out': _L0_cond_in['W_out'], 'L0_ffn_W_gate': _L0_ffn_in['W_gate'], 'L0_ffn_w_gate_proj': _L0_ffn_in['w_gate_proj'], 'L0_ffn_w_up_proj': _L0_ffn_in['w_up_proj'], 'L0_ffn_w_down_proj': _L0_ffn_in['w_down_proj']}

def reference(x, cond_2048, L0_cond_W_emb, L0_cond_b_emb, L0_cond_g_norm, L0_cond_W_qkv, L0_cond_g_q, L0_cond_g_k, L0_cond_W_out, L0_ffn_W_gate, L0_ffn_w_gate_proj, L0_ffn_w_up_proj, L0_ffn_w_down_proj):
    import jax
    import jax.numpy as jnp

    def _L0_cond_ref(x, emb, W_emb, b_emb, g_norm, W_qkv, g_q, g_k, W_out):
        import jax, jax.numpy as jnp
        import numpy as np
        HEADS = 16
        EPS = 1e-06

        def _rms_norm(x, g):
            xf = x.astype(jnp.float32)
            y = xf * jax.lax.rsqrt(jnp.mean(xf * xf, axis=-1, keepdims=True) + EPS)
            return y.astype(x.dtype) * g
        b, n, dim = x.shape
        h = HEADS
        d = dim // h
        scale_shift = emb @ W_emb + b_emb
        scale, shift = jnp.split(scale_shift, 2, axis=-1)
        xn = _rms_norm(x, g_norm) * (1.0 + scale) + shift
        qkv = xn @ W_qkv
        qkv = qkv.reshape(b, n, 3, h, d)
        q, k, v = jnp.moveaxis(qkv, 2, 0)
        q = jnp.swapaxes(q, 1, 2)
        k = jnp.swapaxes(k, 1, 2)
        v = jnp.swapaxes(v, 1, 2)
        q = _rms_norm(q, g_q)
        k = _rms_norm(k, g_k)
        logits = jnp.einsum('bhqd,bhkd->bhqk', q, k) * d ** (-0.5)
        attn = jax.nn.softmax(logits, axis=-1)
        o = jnp.einsum('bhqk,bhkd->bhqd', attn, v)
        o = jnp.swapaxes(o, 1, 2).reshape(b, n, dim)
        return o + o @ W_out

    def _L0_ffn_ref(hidden_states, W_gate, w_gate_proj, w_up_proj, w_down_proj):
        import jax, jax.numpy as jnp
        import numpy as np
        TOP_K = 2
        'DeepSeek MoE forward: softmax gate -> top-k routing -> SwiGLU experts\n            -> weighted combine + residual. Experts evaluated densely [T,E,*] and the\n            top-k outputs gathered, which is mathematically identical to the masked\n            per-expert loop in the original torch code.'
        B, S, D = hidden_states.shape
        identity = hidden_states
        x = hidden_states.reshape(-1, D)
        scores = jax.nn.softmax(x @ W_gate.T, axis=-1)
        topk_w, topk_i = jax.lax.top_k(scores, TOP_K)
        topk_w = topk_w / jnp.sum(topk_w, axis=-1, keepdims=True)
        g = jax.nn.silu(jnp.einsum('td,edh->teh', x, w_gate_proj))
        u = jnp.einsum('td,edh->teh', x, w_up_proj)
        eo = jnp.einsum('teh,ehd->ted', g * u, w_down_proj)
        sel = jnp.take_along_axis(eo, topk_i[:, :, None], axis=1)
        y = jnp.sum(sel * topk_w[:, :, None].astype(eo.dtype), axis=1)
        return y.reshape(B, S, D) + identity
    x = x + _L0_ffn_ref(_L0_cond_ref(x, cond_2048[:, None, :], L0_cond_W_emb, L0_cond_b_emb, L0_cond_g_norm, L0_cond_W_qkv, L0_cond_g_q, L0_cond_g_k, L0_cond_W_out), L0_ffn_W_gate, L0_ffn_w_gate_proj, L0_ffn_w_up_proj, L0_ffn_w_down_proj)
    return x

_drawn_inputs = setup_inputs


def setup_inputs(seed=0):
    import zlib

    import numpy as np

    out = dict(_drawn_inputs(seed))
    spreads = {'L0_cond_b_emb': (0.0, 0.1),
     'L0_cond_g_norm': (1.0, 0.2),
     'L0_cond_g_q': (1.0, 0.2),
     'L0_cond_g_k': (1.0, 0.2)}
    factors = {}
    for name, (base, spread) in spreads.items():
        noise = np.random.default_rng([zlib.crc32(name.encode()), seed]).standard_normal(out[name].shape)
        drawn = base * np.exp(spread * noise) if base else spread * noise
        out[name] = jnp.asarray(drawn.astype(out[name].dtype))
    for name, factor in factors.items():
        out[name] = (out[name] * factor).astype(out[name].dtype)
    return out
```

```python
from contextlib import ExitStack

import concourse.bass as bass
from concourse import mybir

ALU = mybir.AluOpType
ACT = mybir.ActivationFunctionType
AX = mybir.AxisListType
F32 = mybir.dt.float32
F32R = mybir.dt.float32r
I32 = mybir.dt.int32
U32 = mybir.dt.uint32
ds = bass.ds

P = 128
EPS = 1e-6
TOP_K = 2
SOFTMAX_SAFE = 80.0
RSQRT_MAGIC = float(0x5F3759DF)


class Signal:

    def __init__(self, sem, per, start=0):
        self.sem, self.per, self.start = sem, per, start

    def at(self, b, k):
        return b * self.per + k + self.start


def need(eng, signal, b, k):
    value = signal.at(b, k)
    if isinstance(value, int) and value <= signal.start:
        return
    eng.wait_ge(signal.sem, value)


class Chain:

    def __init__(self, eng, sem, per):
        self.eng = eng
        self.begin(sem, per)

    def begin(self, sem, per):
        self.sem, self.per, self.base, self.n = sem, per, 0, 0

    def open(self, b):
        self.base, self.n = b * self.per, 0

    def link(self, ins):
        ins.then_inc(self.sem, 1)
        self.n += 1

    def settle(self):
        self.eng.wait_ge(self.sem, self.base + self.n)

    def close(self):
        assert self.n <= self.per, (self.n, self.per)
        if self.n < self.per:
            if self.n or not isinstance(self.base, int) or self.base:
                self.settle()
            self.eng.sem_inc(self.sem, self.per - self.n)


def bcast(ap, axis, n):
    dims = [list(x) for x in ap.ap]
    dims.insert(axis, [0, n])
    return bass.AP(ap.tensor, ap.offset, dims)


def adaln_moe_kernel(nc, x, cond, w_emb, b_emb, g_norm, w_qkv, g_q, g_k, w_out,
                     w_gate, w_gp, w_up, w_dn, out):
    B, N, D = x.shape
    E, _, H = w_gp.shape
    DH = g_q.shape[0]
    HEADS = D // DH
    T = N // P
    C = D // P
    TOK = B * N
    G = HEADS // 4
    HC = H // P
    PIECES = C + HC
    WOC = D + E
    HALF = WOC // 2
    BPE = TOK // P
    MAX_BLOCKS = (TOP_K * TOK - E) // P + E
    PARTS = 3 * DH
    NSLOT = 5
    assert (T, C, G, HC, D, 2 * H, DH, E) == (2, 4, 4, 2, 512, 512, 32, 8)

    h_rows = nc.dram_tensor("h_rows", (TOK + P, D), F32).ap()
    w_parts = nc.dram_tensor("w_parts", (E, P, 2, PIECES, D), F32).ap()

    ctx = ExitStack()
    with ctx:
        def sb(name, shape, dt=F32, stack=ctx):
            return stack.enter_context(nc.sbuf_tensor(name, [P, *shape], dt))

        def sem(name):
            return ctx.enter_context(nc.semaphore(name))

        ps_p = ctx.enter_context(nc.psum_tensor("ps_p", [P, 2, 512], F32))
        ps_t = ctx.enter_context(nc.psum_tensor("ps_t", [P, 2, 512], F32))
        ps_s = ctx.enter_context(nc.psum_tensor("ps_s", [P, 2, 512], F32))
        ps_v = ctx.enter_context(nc.psum_tensor("ps_v", [P, 2, 512], F32))

        ident_r = sb("ident_r", [P], F32R)
        ident = ident_r[:].bitcast(F32)
        iota = sb("iota", [P])
        tab = sb("tab", [3, P])
        base = sb("base", [E])
        tab_id = sb("tab_id", [P + 1], I32)
        tab_w = sb("tab_w", [P + 1])
        spare_row = sb("spare_row", [1])
        sched = sb("sched", [3, MAX_BLOCKS], I32)
        free_at = sb("free_at", [E], I32)
        n_i = sb("n_i", [E], I32)

        pa = ExitStack()
        A = lambda name, shape, dt=F32: sb(name, shape, dt, pa)
        wq_hi = A("wq_hi", [C, 3 * D], F32R)
        wq_lo = A("wq_lo", [C, 3 * D], F32R)
        wo_hi = A("wo_hi", [C, WOC], F32R)
        wo_lo = A("wo_lo", [C, WOC], F32R)
        stage = A("stage", [12 * 512])
        probs = stage[:, 0:4096].rearrange("p (r n) -> p r n", r=8)
        qk_raw = stage[:, 4096:6144].rearrange("p (u n) -> p u n", u=4)
        wq_raw = stage[:, :].rearrange("p (c n) -> p c n", c=C)
        tmp = ExitStack()
        wemb = sb("wemb", [C, 2 * D], F32, tmp)
        wout = sb("wout", [C, D], F32, tmp)
        woutT = sb("woutT", [C, D], F32, tmp)
        wpr = sb("wpr", [C, WOC], F32, tmp)
        emb = sb("emb", [D], F32, tmp)
        vecs = sb("vecs", [P], F32, tmp)
        wgate = sb("wgate", [D], F32, tmp)
        g_row = sb("g_row", [3, DH], F32, tmp)
        eye = sb("eye", [P], F32, tmp)
        tmp.close()
        q_cat = [A(f"q_cat{s}", [T, HEADS, PARTS], F32R) for s in range(2)]
        k_cat = [A(f"k_cat{s}", [T, HEADS, PARTS], F32R) for s in range(2)]
        x_in = A("x_in", [T, D])
        xn = A("xn", [T * D])
        xr_v = xn[:, :].rearrange("p (t d) -> p t d", t=T)
        xn_v = xn[:, :].rearrange("p (c n) -> p c n", c=C)
        x_hi = A("x_hi", [C, N], F32R)
        x_lo = A("x_lo", [C, N], F32R)
        sq = A("sq", [2, D])
        work = sq[:].rearrange("p a n -> p (a n)")
        sched_ge = work[:, 0:MAX_BLOCKS * E].rearrange("p (b e) -> p b e", e=E)
        sched_t = work[:, 512:512 + 4 * MAX_BLOCKS].rearrange("p (a b) -> p a b", a=4)
        sched_f = work[:, 768:768 + 4 * E].rearrange("p (a e) -> p a e", a=4)
        v_sb = A("v_sb", [T, D])
        stk = A("stk", [4, 512], F32R)
        o_f = A("o_f", [2, N])
        o_hi = A("o_hi", [G, N], F32R)
        o_lo = A("o_lo", [G, N], F32R)
        h_sb = A("h_sb", [T, WOC])
        xres = A("xres", [T, D])
        tri = A("tri", [P], F32R)
        ones_r = A("ones_r", [P], F32R)
        ones_f = ones_r[:].bitcast(F32)
        gains = A("gains", [DH])
        a_mod = A("a_mod", [C, B])
        s_mod = A("s_mod", [C, B])
        embT = A("embT", [C, B])
        vecT = A("vecT", [12])
        wgT = A("wgT", [C, E])
        g_max = A("g_max", [2])
        shift = A("shift", [1])
        st_x = A("st_x", [5, T])
        st_q = A("st_q", [2, 4, 2 * HEADS])
        st_s = A("st_s", [2, 2 * HEADS])
        top_v = A("top_v", [T, 8])
        top_i = A("top_i", [T, 8], U32)
        top_f = A("top_f", [T, 2])
        oh = A("oh", [2, T, E])
        ohr = A("ohr", [2, T, E])
        mask = A("mask", [T, E], F32R)
        ranks = A("ranks", [T, E])
        rt = A("rt", [12, 2, T])
        rt_i = A("rt_i", [3, 2, T], I32)
        w_hi_r = A("w_hi_r", [2, T], F32R)
        tok_c = A("tok_c", [T])
        one_r = A("one_r", [2, P], F32R)
        one_c = A("one_c", [2, 3, P], F32R)
        e_raw = A("e_raw", [2, D])
        e_hi = A("e_hi", [2, D], F32R)
        pa.close()

        pb = ExitStack()
        Bt = lambda name, shape, dt=F32: sb(name, shape, dt, pb)
        w_sl = Bt("w_sl", [NSLOT, 2, PIECES, D], F32R)
        xg = Bt("xg", [2, D])
        xg_hi = Bt("xg_hi", [2, D], F32R)
        xg_lo = Bt("xg_lo", [2, D], F32R)
        sg = Bt("sg", [2, H])
        gu = Bt("gu", [2, H])
        gu_hi = Bt("gu_hi", [2, H], F32R)
        gu_lo = Bt("gu_lo", [2, H], F32R)
        y_sb = Bt("y_sb", [2, D])
        g_idx = Bt("g_idx", [2, 1], I32)
        s_idx = Bt("s_idx", [2, 1], I32)
        w_sel = Bt("w_sel", [2, 1])
        pb.close()

        ld_emb, ld_vecs, ld_wemb, ld_gains = sem("ld_emb"), sem("ld_vecs"), sem("ld_wemb"), sem("ld_gains")
        ld_wqkv, ld_wout, ld_wgate = sem("ld_wqkv"), sem("ld_wout"), sem("ld_wgate")
        consts, zeroed, spare_st = sem("consts"), sem("zeroed"), sem("spare_st")
        pe_setup, dve_setup, act_setup = sem("pe_setup"), sem("dve_setup"), sem("act_setup")
        act_wo = sem("act_wo")
        setup_step = sem("setup_step")
        sp_turn, pool_turn, dve_turn = sem("sp_turn"), sem("pool_turn"), sem("dve_turn")

        sig = lambda name, per: Signal(sem(name), per)
        x_ld, xres_ld = sig("x_ld", 16), sig("xres_ld", 16)
        row_st = [sig(f"row_st{t}", 32) for t in range(T)]
        eraw_ld = [sig(f"eraw_ld{s}", 16 * PIECES) for s in range(2)]
        epart_st = [sig(f"epart_st{s}", 16 * PIECES) for s in range(2)]
        x_sq = sig("x_sq", T)
        xr_ok = sig("xr_ok", T)
        xT_ps = sig("xT_ps", 1)
        xn_ok = sig("xn_ok", C)
        xhi_ok = sig("xhi_ok", 1)
        xlo_ok = sig("xlo_ok", 1)
        U_ps = sig("U_ps", 6)
        U_ev = sig("U_ev", 6)
        qk_sq = sig("qk_sq", 6)
        hs_ok = sig("hs_ok", 4)
        qk_n = sig("qk_n", 4)
        qk_hi = sig("qk_hi", 4)
        qk_lo = sig("qk_lo", 4)
        T_ps = sig("T_ps", HEADS)
        T_ea, T_ed = sig("T_ea", HEADS // 2), sig("T_ed", HEADS // 2)
        S_ps = sig("S_ps", HEADS)
        ex_ok = sig("ex_ok", HEADS)
        V_ps = sig("V_ps", G)
        nrm = sig("nrm", G)
        ohi_ok, olo_ok = sig("ohi_ok", G), sig("olo_ok", G)
        H_ps = sig("H_ps", T)
        H_ev = sig("H_ev", T)
        xh_ok = sig("xh_ok", T)
        ed_ok = sig("ed_ok", 1)
        dif_ok = sig("dif_ok", 1)
        mask_ok = sig("mask_ok", 1)
        Rp_ps = sig("Rp_ps", 1)
        rank_ev = Signal(sem("rank_ev"), 1, start=1)
        hot_ok = sig("hot_ok", 4)
        Rt_ps = sig("Rt_ps", 4)
        tab_ev = Signal(sem("tab_ev"), 1, start=1)
        ehi_ok, elo_ok = sig("ehi_ok", PIECES), sig("elo_ok", PIECES)
        dve_step = sem("dve_step")
        DVE_STEPS = 80

        sched_ok, tabs_ok = sem("sched_ok"), sem("tabs_ok")
        w_ld = sem("w_ld")
        blk = lambda name, per=1: sig(name, per)
        col_ok = blk("col_ok", 1)
        xg_ld = [blk(f"xg_ld{s}", 8) for s in range(2)]
        xgT_ps, xgh_ok, xgl_ok = blk("xgT_ps"), blk("xgh_ok"), blk("xgl_ok")
        gu_ps = blk("gu_ps")
        e_ok = blk("e_ok")
        gu_ok = blk("gu_ok")
        gT_ps, gh_ok, gl_ok = blk("gT_ps"), blk("gh_ok"), blk("gl_ok")
        y_ps = Signal(sem("y_ps"), 1, start=1)
        wsel_ok = blk("wsel_ok", 2)
        y_ok = blk("y_ok")
        acc_st = blk("acc_st", 16)
        blk_step = sem("blk_step")

        U_TILE = [0, 0, 1, 1, 0, 1]
        U_KIND = [0, 1, 0, 1, 2, 2]
        U_BANK = [0, 1, 1, 0, 0, 1]

        block = ctx.enter_context(nc.Block())

        @block.sync
        def _(sp):
            def rows(t, b):
                return x[ds(b, 1), t * P:(t + 1) * P, :].rearrange("a p d -> p (a d)")

            def load_x(b):
                need(sp, x_sq, b - 1, T)
                need(sp, xr_ok, b - 1, T)
                sp.dma_start(x_in[:], x[ds(b, 1)].rearrange("a (t p) d -> p (a t) d", p=P)).then_inc(x_ld.sem, 16)

            def load_residual(b):
                for t in range(T):
                    need(sp, row_st[t], b - 1, 32)
                sp.dma_start(xres[:], x[ds(b, 1)].rearrange("a (t p) d -> p (a t) d", p=P)).then_inc(xres_ld.sem, 16)

            def load_piece(e, p):
                s, k = p % 2, p // 2
                need(sp, epart_st[s], e, 32 * k)
                if p < C:
                    srcs = [w[ds(e, 1), p * P:(p + 1) * P, :] for w in (w_gp, w_up)]
                else:
                    m = p - C
                    srcs = [w_dn[ds(e, 1), m * P:(m + 1) * P, i * H:(i + 1) * H] for i in range(2)]
                for i, src in enumerate(srcs):
                    sp.dma_start(e_raw[:, s, i * H:(i + 1) * H], src.rearrange("a p h -> p (a h)")).then_inc(eraw_ld[s].sem, 16)

            def store_piece(e, p):
                s = p % 2
                need(sp, elo_ok, e, p + 1)
                sp.dma_start(w_parts[ds(e, 1), :, 0, p, :].rearrange("a p d -> p (a d)"), e_hi[:, s, :].bitcast(F32)).then_inc(epart_st[s].sem, 16)
                sp.dma_start(w_parts[ds(e, 1), :, 1, p, :].rearrange("a p d -> p (a d)"), e_raw[:, s, :]).then_inc(epart_st[s].sem, 16)

            sp.dma_start(emb[0:B, :], cond).then_inc(ld_emb, 16)
            sp.dma_start(vecs[0:8, :], b_emb.rearrange("(a p) -> a p", p=P)).then_inc(ld_vecs, 16)
            sp.dma_start(vecs[8:12, :], g_norm.rearrange("(a p) -> a p", p=P)).then_inc(ld_vecs, 16)
            sp.dma_start(wgate[0:E, :], w_gate).then_inc(ld_wgate, 16)
            load_x(0)
            sp.dma_start(g_row[0:1, 0, :], g_q.rearrange("(a d) -> a d", a=1)).then_inc(ld_gains, 16)
            sp.dma_start(g_row[0:1, 1, :], g_k.rearrange("(a d) -> a d", a=1)).then_inc(ld_gains, 16)
            sp.dma_start(wemb[:], w_emb.rearrange("(c p) n -> p c n", p=P)).then_inc(ld_wemb, 16)
            sp.dma_start(wout[:], w_out.rearrange("(c p) n -> p c n", p=P)).then_inc(ld_wout, 16)
            sp.dma_start(wq_raw, w_qkv.rearrange("(c p) n -> p c n", p=P)).then_inc(ld_wqkv, 16)
            sp.wait_ge(zeroed, 1)
            sp.dma_start(h_rows[TOK:TOK + P], xres[:, 0, :]).then_inc(spare_st, 16)
            sp.dma_start(out[TOK:TOK + P], xres[:, 0, :]).then_inc(spare_st, 16)
            load_x(1)
            sp.wait_ge(spare_st, 32)

            def step(b, ahead):
                if ahead:
                    load_x(b + 2)
                load_residual(b)
                load_piece(b, 0)
                load_piece(b, 1)
                for p in range(PIECES):
                    store_piece(b, p)
                    if p + 2 < PIECES:
                        load_piece(b, p + 2)
                for t in range(T):
                    r = ds(b * N + t * P, P)
                    need(sp, H_ev, b, t + 1)
                    sp.dma_start(h_rows[r], h_sb[:, t, 0:D]).then_inc(row_st[t].sem, 16)
                    need(sp, xh_ok, b, t + 1)
                    sp.dma_start(out[r], xres[:, t, :]).then_inc(row_st[t].sem, 16)
                sp.sem_inc(sp_turn, 1)

            step(0, True)
            with sp.Fori(1, B - 2) as b:
                step(b, True)
            step(B - 2, False)
            step(B - 1, False)

            def load_expert(e):
                if e < NSLOT:
                    if e == 0:
                        need(sp, U_ps, B - 1, 6)
                        for s in range(2):
                            need(sp, epart_st[s], B - 1, 16 * PIECES)
                    if e == 2:
                        sp.wait_ge(tabs_ok, 1)
                        for t in range(T):
                            need(sp, row_st[t], B - 1, 32)
                else:
                    last = sp.value_load(free_at[0:1, e - NSLOT:e - NSLOT + 1], min_val=1, max_val=MAX_BLOCKS + 1)
                    sp.wait_ge(y_ps.sem, last)
                sp.dma_start(w_sl[:, e % NSLOT].bitcast(F32), w_parts[e]).then_inc(w_ld, 16)
                sp.wait_ge(w_ld, 16 * (e + 1))

            for e in range(E):
                load_expert(e)
            need(sp, acc_st, MAX_BLOCKS - 1, 16)

        @block.tensor
        def _(pe):
            def split_mm(o, l_hi, l_lo, r_hi, r_lo, first, last):
                pe.matmul(o, l_hi, r_hi, start=first, stop=False)
                pe.matmul(o, l_lo, r_hi, start=False, stop=False)
                return pe.matmul(o, l_hi, r_lo, start=False, stop=last)

            def transpose_x(b):
                need(pe, xr_ok, b, T)
                for c in range(C):
                    for t in range(T):
                        o = (c % 2) * N + t * P
                        last = pe.transpose(ps_t[:, c // 2, o:o + P], xr_v[:, t, c * P:(c + 1) * P], ident)
                last.then_inc(xT_ps.sem, 1)

            def unit_part(b, u, c):
                t, kind = U_TILE[u], U_KIND[u]
                if c == 0 and u == 0:
                    need(pe, xhi_ok, b, 1)
                    need(pe, xlo_ok, b, 1)
                o = ps_p[:, U_BANK[u], :]
                r = slice(t * P, (t + 1) * P)
                n = slice(kind * D, (kind + 1) * D)
                last = split_mm(o, x_hi[:, c, r], x_lo[:, c, r], wq_hi[:, c, n], wq_lo[:, c, n],
                                c == 0, c == C - 1)
                if c == C - 1:
                    last.then_inc(U_ps.sem, 1)

            def stack(b, s, h):
                if h == 0:
                    need(pe, qk_hi, b, 4)
                    need(pe, qk_lo, b, 4)
                if h >= 2:
                    need(pe, T_ea if h % 2 == 0 else T_ed, b, h // 2)
                for i, cat in enumerate((q_cat[s], k_cat[s])):
                    for t in range(T):
                        o = i * N + t * P
                        last = pe.transpose(ps_t[0:PARTS, h % 2, o:o + P].bitcast(F32R), cat[:, t, h, :], ident_r[:])
                last.then_inc(T_ps.sem, 1)

            def scores(b, h):
                need(pe, T_ea if h % 2 == 0 else T_ed, b, h // 2 + 1)
                need(pe, ex_ok, b, h - 1)
                k = stk[0:PARTS, h % 4, :]
                for i in range(T):
                    last = pe.matmul(ps_s[:, h % 2, i * N:(i + 1) * N], k[:, N + i * P:N + (i + 1) * P],
                                     k[:, 0:N], start=True, stop=True)
                last.then_inc(S_ps.sem, 1)

            def values(b, g, step):
                if step == 0:
                    need(pe, ex_ok, b, 4 * g + 4)
                    need(pe, U_ev, b, 6)
                    need(pe, nrm, b, g - 1)
                i = step % 2
                for j in range(4):
                    h = 4 * g + j
                    q = slice(32 * j, 32 * j + 32)
                    lhs = v_sb[:, i, h * DH:(h + 1) * DH] if step < 2 else ones_f[:, 0:DH]
                    o = (step // 2) * N
                    last = pe.matmul(ps_v[q, g % 2, o:o + N], lhs, probs[:, h % 8, i * N:(i + 1) * N],
                                     start=(i == 0), stop=(i == 1))
                if step == 3:
                    last.then_inc(V_ps.sem, 1)

            def out_proj(b, t):
                r = slice(t * P, (t + 1) * P)
                if t == 0:
                    need(pe, ohi_ok, b, G)
                    need(pe, olo_ok, b, G)
                else:
                    need(pe, H_ev, b, t)
                for c in range(C):
                    for i in range(2):
                        n = slice(i * HALF, (i + 1) * HALF)
                        last = split_mm(ps_p[:, i, 0:HALF], o_hi[:, c, r], o_lo[:, c, r],
                                        wo_hi[:, c, n], wo_lo[:, c, n], c == 0, c == C - 1)
                last.then_inc(H_ps.sem, 1)

            def rank_sums(b):
                need(pe, mask_ok, b, 1)
                pe.matmul(ps_p[:, 0, 0:E], tri[:], mask[:, 0, :], start=True, stop=True)
                pe.matmul(ps_p[:, 0, E:2 * E], tri[:], mask[:, 1, :], start=True, stop=False)
                pe.matmul(ps_p[:, 0, E:2 * E], ones_r[:], mask[:, 0, :], start=False, stop=True)
                pe.matmul(ps_p[:, 0, 2 * E:3 * E], ones_r[:], mask[:, 0, :], start=True, stop=False)
                pe.matmul(ps_p[:, 0, 2 * E:3 * E], ones_r[:], mask[:, 1, :], start=False, stop=True).then_inc(Rp_ps.sem, 1)

            def table_sums(b, i0):
                for i in range(i0, i0 + 2):
                    need(pe, hot_ok, b, i + 1)
                    pe.matmul(ps_p[:, 1, 0:3 * P], one_r[:, i % 2, :], one_c[:, i % 2].rearrange("p a n -> p (a n)"),
                              start=(i == 0), stop=(i == 3)).then_inc(Rt_ps.sem, 1)

            pe.wait_ge(consts, 6)
            pe.wait_ge(ld_emb, 16)
            pe.wait_ge(ld_vecs, 32)
            pe.wait_ge(ld_wgate, 16)
            for c in range(C):
                pe.transpose(ps_p[:, 0, c * B:(c + 1) * B], emb[0:B, c * P:(c + 1) * P], ident[0:B, 0:B])
            pe.transpose(ps_p[:, 0, 64:76], vecs[0:12, :], ident[0:12, 0:12])
            for c in range(C):
                last = pe.transpose(ps_p[:, 0, 128 + c * E:128 + (c + 1) * E], wgate[0:E, c * P:(c + 1) * P], ident[0:E, 0:E])
            last.then_inc(pe_setup, 1)
            pe.wait_ge(dve_setup, 1)
            pe.wait_ge(ld_wemb, 16)
            for n in range(2 * C):
                for k in range(C):
                    last = pe.matmul(ps_p[:, 1, n * B:(n + 1) * B], wemb[:, k, n * P:(n + 1) * P], embT[:, k, :],
                                     start=(k == 0), stop=(k == C - 1))
            last.then_inc(pe_setup, 1)
            pe.wait_ge(dve_setup, 3)
            pe.matmul(ps_s[:, 0, 0:DH], ones_f[0:1, :], g_row[0:1, 2, :], start=True, stop=True).then_inc(pe_setup, 1)
            for n in range(C):
                if n >= 2:
                    pe.wait_ge(dve_setup, 4 + n - 2)
                for m in range(C):
                    last = pe.transpose(ps_v[:, n % 2, m * P:(m + 1) * P], wout[:, m, n * P:(n + 1) * P], ident)
                last.then_inc(pe_setup, 1)
            pe.wait_ge(dve_setup, 7)
            for m in range(C):
                for n in range(C):
                    last = pe.matmul(ps_s[:, 1, m * E:(m + 1) * E], woutT[:, n, m * P:(m + 1) * P], wgT[:, n, :],
                                     start=(n == 0), stop=(n == C - 1))
            last.then_inc(pe_setup, 1)

            transpose_x(0)
            pe.wait_ge(act_setup, 4)
            pe.wait_ge(dve_setup, 13)
            for u in range(6):
                if u >= 2:
                    need(pe, U_ev, 0, [0, 0, 2, 1, 4, 3][u])
                for c in range(C):
                    unit_part(0, u, c)
            need(pe, xn_ok, 0, C)
            transpose_x(1)
            pe.wait_ge(act_wo, 2)
            pe.wait_ge(dve_setup, 14)

            def step(b, s, nxt, ahead, routed):
                n = b + 1
                if nxt:
                    need(pe, xn_ok, n, C // 2)
                else:
                    need(pe, T_ea, b - 1, 8)
                    need(pe, T_ed, b - 1, 8)
                stack(b, s, 0)
                if nxt:
                    need(pe, xn_ok, n, C)
                stack(b, s, 1)
                for g in range(G):
                    for j in range(4):
                        h = 4 * g + j
                        scores(b, h)
                        if h + 2 < HEADS:
                            stack(b, s, h + 2)
                        if nxt:
                            if j == 0:
                                if g == 0 or g == 1:
                                    need(pe, H_ev, b - 1, T)
                                elif g == 2:
                                    need(pe, U_ev, n, 2)
                                elif routed:
                                    need(pe, rank_ev, b - 1, 1)
                                else:
                                    need(pe, U_ev, n, 1)
                            unit_part(n, g, j)
                        if g >= 1:
                            values(b, g - 1, j)
                    if routed and g == 1:
                        if nxt:
                            need(pe, U_ev, n, 1)
                        else:
                            need(pe, H_ev, b - 1, T)
                        rank_sums(b - 1)
                    if routed and g == 3:
                        if nxt:
                            need(pe, U_ev, n, 3)
                        table_sums(b - 1, 0)
                for j in range(4):
                    values(b, G - 1, j)
                if routed:
                    table_sums(b - 1, 2)
                if nxt:
                    need(pe, U_ev, n, 4)
                    for c in range(C):
                        unit_part(n, 4, c)
                    if routed:
                        need(pe, tab_ev, b - 1, 1)
                    else:
                        need(pe, U_ev, n, 3)
                    for c in range(C):
                        unit_part(n, 5, c)
                if ahead:
                    need(pe, T_ea, b, 8)
                    need(pe, T_ed, b, 8)
                    transpose_x(b + 2)
                if nxt:
                    need(pe, U_ev, n, 6)
                else:
                    need(pe, rank_ev, b - 1, 1)
                    need(pe, tab_ev, b - 1, 1)
                for t in range(T):
                    out_proj(b, t)

            step(0, 0, True, True, False)
            with pe.Fori(0, (B - 2) // 2 - 1) as j:
                step(2 * j + 1, 1, True, True, True)
                step(2 * j + 2, 0, True, True, True)
            step(B - 3, 1, True, True, True)
            step(B - 2, 0, True, False, True)
            step(B - 1, 1, False, False, True)
            need(pe, H_ev, B - 1, T)
            rank_sums(B - 1)
            table_sums(B - 1, 0)
            table_sums(B - 1, 2)

            pe.sem_inc(y_ps.sem, 1)
            pe.wait_ge(sched_ok, 1)

            def rows_T(k, s):
                need(pe, xg_ld[s], k, 16 - 8 * s)
                need(pe, xgl_ok, k - 2, 1)
                for c in range(C):
                    last = pe.transpose(ps_t[:, s, c * P:(c + 1) * P], xg[:, s, c * P:(c + 1) * P], ident)
                last.then_inc(xgT_ps.sem, 1)

            def slot_of(k):
                return pe.value_load(sched[0:1, 1, ds(k, 1)], min_val=0, max_val=NSLOT - 1)

            def gate_up(k, s):
                e = pe.value_load(sched[0:1, 2, ds(k, 1)], min_val=16, max_val=16 * E)
                w = slot_of(k)
                pe.wait_ge(w_ld, e)
                need(pe, xgh_ok, k, 1)
                need(pe, xgl_ok, k, 1)
                need(pe, gu_ok, k - 2, 1)
                o = ps_p[:, s, :]
                for c in range(C):
                    n = slice(c * P, (c + 1) * P)
                    hi = w_sl[:, ds(w, 1), 0, c, :].rearrange("p a n -> p (a n)")
                    lo = w_sl[:, ds(w, 1), 1, c, :].rearrange("p a n -> p (a n)")
                    last = split_mm(o, xg_hi[:, s, n], xg_lo[:, s, n], hi, lo, c == 0, c == C - 1)
                last.then_inc(gu_ps.sem, 1)

            def act_T(k, s):
                need(pe, gu_ok, k, 1)
                need(pe, gl_ok, k - 2, 1)
                for c in range(HC):
                    last = pe.transpose(ps_v[:, s, c * P:(c + 1) * P], gu[:, s, c * P:(c + 1) * P], ident)
                last.then_inc(gT_ps.sem, 1)

            def down(k, s):
                w = slot_of(k)
                need(pe, gh_ok, k, 1)
                need(pe, gl_ok, k, 1)
                need(pe, y_ok, k - 2, 1)
                o = ps_s[:, s, :]
                for c in range(HC):
                    n = slice(c * P, (c + 1) * P)
                    hi = w_sl[:, ds(w, 1), 0, C + c, :].rearrange("p a n -> p (a n)")
                    lo = w_sl[:, ds(w, 1), 1, C + c, :].rearrange("p a n -> p (a n)")
                    last = split_mm(o, gu_hi[:, s, n], gu_lo[:, s, n], hi, lo, c == 0, c == HC - 1)
                last.then_inc(y_ps.sem, 1)

            def blk_stage(k, par, lo=0, hi=MAX_BLOCKS):
                if not isinstance(k, int) or k + 1 < MAX_BLOCKS and k + 1 >= 0:
                    gate_up(k + 1, (par + 1) % 2)
                if not isinstance(k, int) or 0 <= k < MAX_BLOCKS:
                    act_T(k, par)
                if not isinstance(k, int) or k + 3 < MAX_BLOCKS:
                    rows_T(k + 3, (par + 1) % 2)
                if not isinstance(k, int) or 0 <= k - 1:
                    down(k - 1, (par + 1) % 2)

            for k in range(-3, 3):
                blk_stage(k, k % 2)
            pairs = (MAX_BLOCKS - 3 - 3) // 2
            with pe.Fori(0, pairs) as j:
                blk_stage(2 * j + 3, 1)
                blk_stage(2 * j + 4, 0)
            for k in range(3 + 2 * pairs, MAX_BLOCKS + 1):
                blk_stage(k, k % 2)

        @block.scalar
        def _(act):
            def unit_out(b, u):
                need(act, U_ps, b, u + 1)
                t, kind = U_TILE[u], U_KIND[u]
                if kind == 2:
                    need(act, V_ps, b - 1, G)
                    dst = v_sb[:, t, :]
                else:
                    need(act, qk_hi, b - 1, u + 1)
                    need(act, qk_lo, b - 1, u + 1)
                    dst = qk_raw[:, u, :]
                act.copy(dst, ps_p[:, U_BANK[u], :]).then_inc(U_ev.sem, 1)

            def parts_hi(b, s, u):
                need(act, qk_n, b, u + 1)
                need(act, T_ps, b - 2, HEADS)
                t = U_TILE[u]
                src = bcast(qk_raw[:, u, :].rearrange("p (h d) -> p h d", d=DH), 2, 2)
                if U_KIND[u] == 0:
                    dst = q_cat[s][:, t].rearrange("p h (r d) -> p h r d", d=DH)[:, :, 0:3:2, :]
                else:
                    dst = k_cat[s][:, t].rearrange("p h (r d) -> p h r d", d=DH)[:, :, 0:2, :]
                act.copy(dst, src).then_inc(qk_hi.sem, 1)

            def square_x(b):
                need(act, x_ld, b, 16)
                need(act, xhi_ok, b - 1, 1)
                need(act, xlo_ok, b - 1, 1)
                need(act, xr_ok, b - 1, T)
                for t in range(T):
                    act.activation(xr_v[:, t, :], x_in[:, t, :], ACT.Square,
                                   accum_out=st_x[:, 0, t:t + 1]).then_inc(x_sq.sem, 1)

            def x_hi_part(b):
                need(act, xn_ok, b, C)
                need(act, U_ps, b - 1, 6)
                act.copy(x_hi[:].rearrange("p c n -> p (c n)"), xn[:]).then_inc(xhi_ok.sem, 1)

            def stack_out(b, h):
                need(act, T_ps, b, h + 1)
                need(act, S_ps, b, h - 3)
                act.copy(stk[0:PARTS, h % 4, :], ps_t[0:PARTS, h % 2, :]).then_inc(T_ea.sem, 1)

            def exps(b, h):
                need(act, S_ps, b, h + 1)
                need(act, V_ps, b, h // 4 - 1)
                act.activation(probs[:, h % 8, :], ps_s[:, h % 2, :], ACT.Exp, bias=shift[:, 0:1]).then_inc(ex_ok.sem, 1)

            def out_hi(b, g):
                need(act, nrm, b, g + 1)
                need(act, H_ps, b - 1, T)
                act.copy(o_hi[:, g, :], o_f[:, g % 2, :]).then_inc(ohi_ok.sem, 1)

            def rows_out(b, t):
                need(act, H_ps, b, t + 1)
                need(act, row_st[t], b - 1, 32)
                need(act, xh_ok, b - 1, t + 1)
                need(act, dif_ok, b - 1, 1)
                act.copy(h_sb[:, t, 0:HALF], ps_p[:, 0, 0:HALF])
                act.copy(h_sb[:, t, HALF:WOC], ps_p[:, 1, 0:HALF]).then_inc(H_ev.sem, 1)

            def pick_exp(b):
                need(act, dif_ok, b, 1)
                act.activation(rt[:, 1, 0, :], rt[:, 0, 0, :], ACT.Exp).then_inc(ed_ok.sem, 1)

            square_x(0)
            act.wait_ge(dve_setup, 9)
            act.copy(wo_hi[:, 0:2, :], wpr[:, 0:2, :]).then_inc(act_wo, 1)
            act.copy(wo_hi[:, 2:4, :], wpr[:, 2:4, :]).then_inc(act_wo, 1)
            act.wait_ge(ld_wqkv, 16)
            for c in range(C):
                act.copy(wq_hi[:, c, :], wq_raw[:, c, :]).then_inc(act_setup, 1)
            x_hi_part(0)
            for u in range(4):
                unit_out(0, u)
            square_x(1)
            for u in range(4, 6):
                unit_out(0, u)
            for u in range(4):
                parts_hi(0, 0, u)
            x_hi_part(1)

            def step(b, s, nxt, ahead, routed):
                n, sn = b + 1, 1 - s
                stack_out(b, 0)
                for g in range(G):
                    for j in range(4):
                        h = 4 * g + j
                        if h % 2 == 0 and h + 2 < HEADS:
                            stack_out(b, h + 2)
                        exps(b, h)
                        if g == 0 and j == 2 and routed:
                            pick_exp(b - 1)
                        if g >= 2 and j == 2:
                            out_hi(b, g - 2)
                        if g == 0 and j == 3 and ahead:
                            square_x(b + 2)
                        if g == 3 and j >= 2 and nxt:
                            parts_hi(n, sn, j - 2)
                    if nxt:
                        unit_out(n, g)
                out_hi(b, 2)
                out_hi(b, 3)
                if nxt:
                    unit_out(n, 4)
                    unit_out(n, 5)
                    parts_hi(n, sn, 2)
                    parts_hi(n, sn, 3)
                if ahead:
                    x_hi_part(b + 2)
                rows_out(b, 0)
                rows_out(b, 1)

            step(0, 0, True, True, False)
            with act.Fori(0, (B - 2) // 2 - 1) as j:
                step(2 * j + 1, 1, True, True, True)
                step(2 * j + 2, 0, True, True, True)
            step(B - 3, 1, True, True, True)
            step(B - 2, 0, True, False, True)
            step(B - 1, 1, False, False, True)
            pick_exp(B - 1)

            def rows_hi(k, s):
                need(act, xgT_ps, k, 1)
                need(act, gu_ps, k - 2, 1)
                act.copy(xg_hi[:, s, :], ps_t[:, s, :]).then_inc(xgh_ok.sem, 1)

            def gate_exp(k, s):
                need(act, gu_ps, k, 1)
                need(act, gu_ok, k - 2, 1)
                act.activation(sg[:, s, :], ps_p[:, s, 0:H], ACT.Exp, scale=-1.0).then_inc(e_ok.sem, 1)

            def act_hi(k, s):
                need(act, gT_ps, k, 1)
                need(act, y_ps, k - 2, 1)
                act.copy(gu_hi[:, s, :], ps_v[:, s, 0:H]).then_inc(gh_ok.sem, 1)

            def rows_weighted(k, s):
                need(act, y_ps, k, 1)
                need(act, wsel_ok, k, 2)
                need(act, acc_st, k - 2, 16)
                act.activation(y_sb[:, s, :], ps_s[:, s, :], ACT.Copy, scale=w_sel[:, s, :]).then_inc(y_ok.sem, 1)

            act.wait_ge(tabs_ok, 1)

            def blk_stage(k, par):
                if not isinstance(k, int) or k + 1 < MAX_BLOCKS and k + 1 >= 0:
                    gate_exp(k + 1, (par + 1) % 2)
                if not isinstance(k, int) or 0 <= k < MAX_BLOCKS:
                    act_hi(k, par)
                if not isinstance(k, int) or k + 3 < MAX_BLOCKS:
                    rows_hi(k + 3, (par + 1) % 2)
                if not isinstance(k, int) or 0 <= k - 1:
                    rows_weighted(k - 1, (par + 1) % 2)

            for k in range(-3, 3):
                blk_stage(k, k % 2)
            pairs = (MAX_BLOCKS - 3 - 3) // 2
            with act.Fori(0, pairs) as j:
                blk_stage(2 * j + 3, 1)
                blk_stage(2 * j + 4, 0)
            for k in range(3 + 2 * pairs, MAX_BLOCKS + 1):
                blk_stage(k, k % 2)

        @block.vector
        def _(dve):
            chain = Chain(dve, setup_step, 0)

            def rsqrt(var, y, z):
                chain.link(dve.tensor_scalar(y.bitcast(I32), var.bitcast(I32), 1, None, ALU.logical_shift_right))
                chain.settle()
                chain.link(dve.tensor_scalar(y.bitcast(I32), y.bitcast(I32), -1.0, RSQRT_MAGIC, ALU.mult, ALU.add))
                chain.settle()
                for _ in range(3):
                    chain.link(dve.scalar_tensor_tensor(z, y, -0.5, y, ALU.mult, ALU.mult))
                    chain.settle()
                    chain.link(dve.tensor_tensor(z, z, var, ALU.mult))
                    chain.settle()
                    chain.link(dve.scalar_tensor_tensor(y, z, 1.5, y, ALU.add, ALU.mult))
                    chain.settle()

            def normalise_x(b):
                need(dve, x_sq, b, T)
                chain.link(dve.tensor_scalar(st_x[:, 1, :], st_x[:, 0, :], 1.0 / D, EPS, ALU.mult, ALU.add))
                chain.settle()
                rsqrt(st_x[:, 1, :], st_x[:, 2, :], st_x[:, 3, :])
                for t in range(T):
                    dve.tensor_scalar(xr_v[:, t, :], x_in[:, t, :], st_x[:, 2, t:t + 1], None,
                                      ALU.mult).then_inc(xr_ok.sem, 1)

            def modulate(b, c0=0):
                need(dve, xT_ps, b, 1)
                for c in range(C):
                    o = (c % 2) * N
                    dve.tensor_scalar(xn_v[:, c, :], ps_t[:, c // 2, o:o + N], a_mod[:, c, ds(b, 1)],
                                      s_mod[:, c, ds(b, 1)], ALU.mult, ALU.add).then_inc(xn_ok.sem, 1)

            def head_sums(b, u):
                t, kind = U_TILE[u], U_KIND[u]
                need(dve, qk_sq, b, [2, 3, 5, 6][u])
                dve.tensor_reduce(st_s[:, t, kind * HEADS:(kind + 1) * HEADS],
                                  sq[:, u % 2, :].rearrange("p (h d) -> p h d", d=DH), AX.X, ALU.add).then_inc(hs_ok.sem, 1)

            def head_scales(b, t):
                need(dve, hs_ok, b, 2 * t + 2)
                chain.link(dve.tensor_scalar(st_q[:, t, 0, :], st_s[:, t, :], 1.0 / DH, EPS, ALU.mult, ALU.add))
                chain.settle()
                rsqrt(st_q[:, t, 0, :], st_q[:, t, 1, :], st_q[:, t, 2, :])

            def scale_heads(b, u):
                t, kind = U_TILE[u], U_KIND[u]
                v = qk_raw[:, u, :].rearrange("p (h d) -> p h d", d=DH)
                r = bcast(st_q[:, t, 1, kind * HEADS:(kind + 1) * HEADS], 2, DH)
                dve.tensor_tensor(v, v, r, ALU.mult).then_inc(qk_n.sem, 1)

            def parts_lo(b, s, u):
                need(dve, qk_hi, b, u + 1)
                t = U_TILE[u]
                cat = (q_cat, k_cat)[U_KIND[u]][s][:, t].rearrange("p h (r d) -> p h r d", d=DH)
                src = qk_raw[:, u, :].rearrange("p (h d) -> p h d", d=DH)
                dve.tensor_tensor(cat[:, :, 1 + U_KIND[u], :], src, cat[:, :, 0, :].bitcast(F32),
                                  ALU.subtract).then_inc(qk_lo.sem, 1)

            def stack_out(b, h):
                need(dve, T_ps, b, h + 1)
                need(dve, S_ps, b, h - 3)
                dve.tensor_copy(stk[0:PARTS, h % 4, :], ps_t[0:PARTS, h % 2, :]).then_inc(T_ed.sem, 1)

            def normalise_out(b, g):
                need(dve, V_ps, b, g + 1)
                need(dve, ohi_ok, b, g - 1)
                need(dve, olo_ok, b, g - 1)
                chain.link(dve.reciprocal(o_f[:, g % 2, :], ps_v[:, g % 2, N:2 * N]))
                chain.settle()
                dve.tensor_tensor(o_f[:, g % 2, :], ps_v[:, g % 2, 0:N], o_f[:, g % 2, :], ALU.mult).then_inc(nrm.sem, 1)

            def out_lo(b, g):
                need(dve, ohi_ok, b, g + 1)
                dve.tensor_tensor(o_lo[:, g, :], o_f[:, g % 2, :], o_hi[:, g, :].bitcast(F32),
                                  ALU.subtract).then_inc(olo_ok.sem, 1)

            def add_rows(b, t):
                need(dve, H_ev, b, t + 1)
                need(dve, xres_ld, b, 16)
                dve.tensor_tensor(xres[:, t, :], xres[:, t, :], h_sb[:, t, 0:D], ALU.add).then_inc(xh_ok.sem, 1)

            def picks(b):
                need(dve, H_ev, b, T)
                dve.sem_inc(dve_turn, 1)
                for t in range(T):
                    chain.link(dve.max(top_v[:, t, :], h_sb[:, t, D:WOC]))
                chain.settle()
                dve.sem_inc(dve_turn, 1)
                for t in range(T):
                    chain.link(dve.max_index(top_i[:, t, :], top_v[:, t, :], h_sb[:, t, D:WOC]))
                chain.settle()
                chain.link(dve.tensor_copy(top_f[:], top_i[:, :, 0:2]))
                dve.tensor_tensor(rt[:, 0, 0, :], top_v[:, :, 1], top_v[:, :, 0], ALU.subtract).then_inc(dif_ok.sem, 1)
                chain.settle()
                picks_f = top_f[:].rearrange("p t s -> p s t")
                chain.link(dve.tensor_tensor(oh[:], bcast(bcast(iota[:, 0:E], 1, T), 1, 2), bcast(picks_f, 3, E), ALU.is_equal))
                chain.link(dve.tensor_scalar(rt[:, 2], picks_f, float(BPE), None, ALU.mult))
                chain.settle()
                dve.tensor_tensor(mask[:], oh[:, 0], oh[:, 1], ALU.add).then_inc(mask_ok.sem, 1)

            def pick_weights(b):
                need(dve, ed_ok, b, 1)
                chain.link(dve.tensor_scalar(rt[:, 3, 0, :], rt[:, 1, 0, :], 1.0, None, ALU.add))
                chain.settle()
                chain.link(dve.reciprocal(rt[:, 4, 0, :], rt[:, 3, 0, :]))
                chain.settle()
                chain.link(dve.tensor_tensor(rt[:, 4, 1, :], rt[:, 1, 0, :], rt[:, 4, 0, :], ALU.mult))
                chain.settle()
                chain.link(dve.tensor_copy(w_hi_r[:], rt[:, 4]))
                chain.settle()
                chain.link(dve.tensor_tensor(rt[:, 5], rt[:, 4], w_hi_r[:].bitcast(F32), ALU.subtract))

            def slots(b):
                need(dve, Rp_ps, b, 1)
                need(dve, rank_ev, b - 1, 1)
                ps = ps_p[:, 0, 0:2 * E].rearrange("p (t e) -> p t e", t=T)
                chain.link(dve.tensor_tensor(ranks[:], ps, bcast(base[:], 1, T), ALU.add))
                chain.settle()
                dve.tensor_tensor(base[:], base[:], ps_p[:, 0, 2 * E:3 * E], ALU.add).then_inc(rank_ev.sem, 1)
                chain.link(dve.tensor_tensor(ohr[:, 0], oh[:, 0], ranks[:], ALU.mult))
                chain.link(dve.tensor_tensor(ohr[:, 1], oh[:, 1], ranks[:], ALU.mult))
                chain.settle()
                chain.link(dve.tensor_reduce(rt[:, 9], ohr[:], AX.X, ALU.add))
                chain.settle()
                chain.link(dve.tensor_copy(rt_i[:, 0], rt[:, 9]))
                chain.settle()
                chain.link(dve.tensor_scalar(rt_i[:, 1], rt_i[:, 0], P - 1, None, ALU.bitwise_and))
                chain.link(dve.tensor_scalar(rt_i[:, 2], rt_i[:, 0], 7, None, ALU.logical_shift_right))
                chain.settle()
                chain.link(dve.tensor_copy(rt[:, 6], rt_i[:, 1]))
                chain.link(dve.tensor_tensor(rt[:, 7], rt_i[:, 2], rt[:, 2], ALU.add))
                chain.settle()
                chain.link(dve.tensor_tensor(rt[:, 8], bcast(tok_c[:], 1, 2), rt[:, 6], ALU.subtract))
                chain.settle()
                chain.link(dve.tensor_scalar(tok_c[:], tok_c[:], float(N), None, ALU.add))

            def one_hots(b, i0):
                for i in range(i0, i0 + 2):
                    k, t = i // 2, i % 2
                    if i >= 2:
                        need(dve, Rt_ps, b, i - 1)
                    row, col = rt[:, 6, k, t:t + 1], rt[:, 7, k, t:t + 1]
                    dve.tensor_scalar(one_r[:, i % 2, :], iota[:], row, None, ALU.is_equal)
                    for m, val in enumerate((rt[:, 8, k, t:t + 1], rt[:, 4, k, t:t + 1], rt[:, 5, k, t:t + 1])):
                        v = w_hi_r[:, k, t:t + 1].bitcast(F32) if m == 1 else val
                        last = dve.tensor_scalar(one_c[:, i % 2, m, :], iota[:], col, v, ALU.is_equal, ALU.mult)
                    last.then_inc(hot_ok.sem, 1)

            def tables(b):
                need(dve, Rt_ps, b, 4)
                need(dve, tab_ev, b - 1, 1)
                t = tab[:].rearrange("p a n -> p (a n)")
                dve.tensor_tensor(t, t, ps_p[:, 1, 0:3 * P], ALU.add).then_inc(tab_ev.sem, 1)

            dve.sem_inc(rank_ev.sem, 1)
            dve.sem_inc(tab_ev.sem, 1)
            dve.memset(ones_r[:].bitcast(F32), 1.0).then_inc(consts, 1)
            dve.memset(xres[:, 0, :], 0.0).then_inc(zeroed, 1)
            dve.memset(tab[:, 1:3, :].rearrange("p a n -> p (a n)"), 0.0)
            dve.memset(base[:], 0.0)
            dve.wait_ge(consts, 5)
            dve.tensor_copy(ident_r[:], eye[:]).then_inc(consts, 1)
            dve.wait_ge(pe_setup, 1)
            dve.tensor_copy(embT[:].rearrange("p c b -> p (c b)"), ps_p[:, 0, 0:C * B])
            dve.tensor_copy(vecT[:], ps_p[:, 0, 64:76])
            dve.tensor_copy(wgT[:].rearrange("p c e -> p (c e)"), ps_p[:, 0, 128:128 + C * E]).then_inc(dve_setup, 1)
            dve.wait_ge(ld_gains, 32)
            chain.link(dve.tensor_tensor(g_row[0:1, 2, :], g_row[0:1, 0, :], g_row[0:1, 1, :], ALU.mult))
            chain.settle()
            dve.tensor_scalar(g_row[0:1, 2, :], g_row[0:1, 2, :], float(DH) ** -0.5, None, ALU.mult).then_inc(dve_setup, 1)
            normalise_x(0)
            dve.wait_ge(ld_wout, 16)
            for c in range(C):
                last = dve.tensor_tensor(wout[:, c, c * P:(c + 1) * P], wout[:, c, c * P:(c + 1) * P], eye[:], ALU.add)
            last.then_inc(dve_setup, 1)
            for n in range(C):
                dve.wait_ge(pe_setup, 4 + n)
                dve.tensor_copy(woutT[:, n, :], ps_v[:, n % 2, :]).then_inc(dve_setup, 1)
            for c in range(C):
                chain.link(dve.tensor_scalar(a_mod[:, c, :], ps_p[:, 1, c * B:(c + 1) * B], vecT[:, c:c + 1], 1.0, ALU.add, ALU.add))
                chain.link(dve.tensor_scalar(s_mod[:, c, :], ps_p[:, 1, (C + c) * B:(C + c + 1) * B], vecT[:, C + c:C + c + 1], None, ALU.add))
            chain.settle()
            for c in range(C):
                last = dve.tensor_scalar(a_mod[:, c, :], a_mod[:, c, :], vecT[:, 8 + c:9 + c], None, ALU.mult)
            last.then_inc(dve_setup, 1)
            chain.link(dve.tensor_copy(gains[:], ps_s[:, 0, 0:DH]))
            chain.settle()
            chain.link(dve.tensor_reduce(g_max[:, 0:1], gains[:], AX.X, ALU.max, apply_absolute_value=True))
            chain.settle()
            chain.link(dve.tensor_scalar(g_max[:, 1:2], g_max[:, 0:1], -float(DH), SOFTMAX_SAFE, ALU.mult, ALU.add))
            chain.settle()
            chain.link(dve.tensor_scalar(shift[:], g_max[:, 1:2], 0.0, None, ALU.min))
            dve.wait_ge(pe_setup, 8)
            dve.tensor_copy(wpr[:, :, 0:D], wout[:])
            dve.tensor_copy(wpr[:, :, D:WOC], ps_s[:, 1, 0:C * E].rearrange("p (c e) -> p c e", c=C)).then_inc(dve_setup, 1)
            dve.wait_ge(dve_setup, 9)
            modulate(0)
            for c in range(C):
                dve.wait_ge(act_setup, c + 1)
                dve.tensor_tensor(wq_lo[:, c, :], wq_raw[:, c, :], wq_hi[:, c, :].bitcast(F32), ALU.subtract).then_inc(dve_setup, 1)
            dve.wait_ge(act_wo, 2)
            dve.tensor_tensor(wo_lo[:], wpr[:], wo_hi[:].bitcast(F32), ALU.subtract).then_inc(dve_setup, 1)
            normalise_x(1)
            for t in range(T):
                head_sums(0, 2 * t)
                head_sums(0, 2 * t + 1)
                head_scales(0, t)
                scale_heads(0, 2 * t)
                scale_heads(0, 2 * t + 1)
            for u in range(4):
                parts_lo(0, 0, u)
            modulate(1)
            chain.begin(dve_step, DVE_STEPS)

            def step(b, s, nxt, ahead, routed):
                n, sn = b + 1, 1 - s
                chain.open(b)
                stack_out(b, 1)
                for g in range(G):
                    for j in range(4):
                        h = 4 * g + j
                        if h % 2 == 1 and h + 2 < HEADS:
                            stack_out(b, h + 2)
                        if routed:
                            if (g, j) == (0, 1):
                                picks(b - 1)
                            if (g, j) == (1, 1):
                                pick_weights(b - 1)
                            if (g, j) == (2, 1):
                                slots(b - 1)
                            if (g, j) == (3, 3):
                                one_hots(b - 1, 0)
                        if (g, j) == (1, 3):
                            if nxt:
                                head_sums(n, 0)
                            if ahead:
                                normalise_x(b + 2)
                        if (g, j) == (2, 1):
                            normalise_out(b, 0)
                        if (g, j) == (2, 3):
                            if nxt:
                                head_sums(n, 1)
                                head_scales(n, 0)
                            out_lo(b, 0)
                        if (g, j) == (3, 1):
                            normalise_out(b, 1)
                            if nxt:
                                scale_heads(n, 0)
                                scale_heads(n, 1)
                        if (g, j) == (3, 3):
                            out_lo(b, 1)
                            if nxt:
                                head_sums(n, 2)
                                parts_lo(n, sn, 0)
                                parts_lo(n, sn, 1)
                normalise_out(b, 2)
                if routed:
                    one_hots(b - 1, 2)
                out_lo(b, 2)
                normalise_out(b, 3)
                if routed:
                    tables(b - 1)
                out_lo(b, 3)
                if nxt:
                    head_sums(n, 3)
                    head_scales(n, 1)
                    scale_heads(n, 2)
                    scale_heads(n, 3)
                    parts_lo(n, sn, 2)
                    parts_lo(n, sn, 3)
                if ahead:
                    modulate(b + 2)
                add_rows(b, 0)
                add_rows(b, 1)
                chain.close()

            step(0, 0, True, True, False)
            with dve.Fori(0, (B - 2) // 2 - 1) as j:
                step(2 * j + 1, 1, True, True, True)
                step(2 * j + 2, 0, True, True, True)
            step(B - 3, 1, True, True, True)
            step(B - 2, 0, True, False, True)
            step(B - 1, 1, False, False, True)
            chain.open(B)
            picks(B - 1)
            pick_weights(B - 1)
            slots(B - 1)
            one_hots(B - 1, 0)
            one_hots(B - 1, 2)
            need(dve, rank_ev, B - 1, 1)
            L, S = chain.link, chain.settle
            nb, cb, gap = sched_f[:, 0, :], sched_f[:, 1, :], sched_f[:, 2, :]
            L(dve.tensor_scalar(n_i[:], base[:], float(P - 1), None, ALU.add)); S()
            L(dve.tensor_scalar(n_i[:], n_i[:], 7, None, ALU.logical_shift_right)); S()
            L(dve.tensor_copy(nb, n_i[:])); S()
            L(dve.tensor_copy(cb, nb))
            L(dve.tensor_scalar(gap, nb, -1.0, float(BPE), ALU.mult, ALU.add)); S()
            for k in (1, 2, 4):
                a, z = (sched_f[:, 1, :], sched_f[:, 3, :]) if k != 2 else (sched_f[:, 3, :], sched_f[:, 1, :])
                L(dve.tensor_tensor(z[:, k:], a[:, k:], a[:, 0:E - k], ALU.add))
                L(dve.tensor_copy(z[:, 0:k], a[:, 0:k])); S()
            cb = sched_f[:, 3, :]
            L(dve.tensor_tensor(sched_ge[:], bcast(iota[:, 0:MAX_BLOCKS], 2, E), bcast(cb, 1, MAX_BLOCKS), ALU.is_ge)); S()
            L(dve.tensor_reduce(sched_t[:, 0, :], sched_ge[:], AX.X, ALU.add)); S()
            L(dve.tensor_tensor(sched_ge[:], sched_ge[:], bcast(gap, 1, MAX_BLOCKS), ALU.mult))
            L(dve.tensor_scalar(sched_t[:, 1, :], sched_t[:, 0, :], float(E - 1), None, ALU.min)); S()
            L(dve.tensor_reduce(sched_t[:, 2, :], sched_ge[:], AX.X, ALU.add))
            L(dve.tensor_scalar(sched_t[:, 3, :], sched_t[:, 1, :], float(NSLOT), float(-NSLOT), ALU.is_ge, ALU.mult)); S()
            L(dve.tensor_tensor(sched_t[:, 2, :], sched_t[:, 2, :], iota[:, 0:MAX_BLOCKS], ALU.add))
            L(dve.tensor_tensor(sched[:, 1, :], sched_t[:, 1, :], sched_t[:, 3, :], ALU.add))
            L(dve.tensor_scalar(sched[:, 2, :], sched_t[:, 1, :], 1.0, 16.0, ALU.add, ALU.mult)); S()
            L(dve.tensor_scalar(sched[:, 0, :], sched_t[:, 2, :], float(P), None, ALU.min))
            dve.tensor_scalar(free_at[:], cb, 1.0, None, ALU.add).then_inc(sched_ok, 1)
            tables(B - 1)
            need(dve, tab_ev, B - 1, 1)
            L(dve.tensor_copy(tab_id[:, 0:P], tab[:, 0, :]))
            L(dve.tensor_tensor(tab_w[:, 0:P], tab[:, 1, :], tab[:, 2, :], ALU.add)); S()
            L(dve.tensor_copy(tab_id[:, P:P + 1], spare_row[:]))
            dve.memset(tab_w[:, P:P + 1], 0.0).then_inc(tabs_ok, 1)
            assert chain.n <= DVE_STEPS

            blkc = Chain(dve, blk_step, 3)

            def swiglu(k, s):
                need(dve, e_ok, k, 1)
                need(dve, gT_ps, k - 2, 1)
                blkc.open(k)
                blkc.link(dve.tensor_scalar(sg[:, s, :], sg[:, s, :], 1.0, None, ALU.add)); blkc.settle()
                blkc.link(dve.reciprocal(sg[:, s, :], sg[:, s, :])); blkc.settle()
                blkc.link(dve.tensor_tensor(sg[:, s, :], ps_p[:, s, 0:H], sg[:, s, :], ALU.mult)); blkc.settle()
                dve.tensor_tensor(gu[:, s, :], ps_p[:, s, H:2 * H], sg[:, s, :], ALU.mult).then_inc(gu_ok.sem, 1)

            def act_lo(k, s):
                need(dve, gh_ok, k, 1)
                dve.tensor_tensor(gu_lo[:, s, :], ps_v[:, s, 0:H], gu_hi[:, s, :].bitcast(F32), ALU.subtract).then_inc(gl_ok.sem, 1)

            def rows_lo(k, s):
                need(dve, xgh_ok, k, 1)
                dve.tensor_tensor(xg_lo[:, s, :], ps_t[:, s, :], xg_hi[:, s, :].bitcast(F32), ALU.subtract).then_inc(xgl_ok.sem, 1)

            def blk_stage(k, par):
                if not isinstance(k, int) or k + 1 < MAX_BLOCKS and k + 1 >= 0:
                    swiglu(k + 1, (par + 1) % 2)
                if not isinstance(k, int) or 0 <= k < MAX_BLOCKS:
                    act_lo(k, par)
                if not isinstance(k, int) or k + 3 < MAX_BLOCKS:
                    rows_lo(k + 3, (par + 1) % 2)

            for k in range(-3, 3):
                blk_stage(k, k % 2)
            pairs = (MAX_BLOCKS - 3 - 3) // 2
            with dve.Fori(0, pairs) as j:
                blk_stage(2 * j + 3, 1)
                blk_stage(2 * j + 4, 0)
            for k in range(3 + 2 * pairs, MAX_BLOCKS + 1):
                blk_stage(k, k % 2)

        @block.gpsimd
        def _(pool):
            def square_unit(b, u):
                need(pool, U_ev, b, u + 1)
                need(pool, hs_ok, b, u - 1)
                pool.tensor_tensor(sq[:, u % 2, :], qk_raw[:, u, :], qk_raw[:, u, :], ALU.mult).then_inc(qk_sq.sem, 1)
                if U_KIND[u] == 0:
                    need(pool, qk_sq, b, [1, 0, 4][u])
                    q = qk_raw[:, u, :].rearrange("p (h d) -> p h d", d=DH)
                    pool.tensor_tensor(q, q, bcast(gains[:], 1, HEADS), ALU.mult).then_inc(qk_sq.sem, 1)

            def x_lo_part(b):
                need(pool, xhi_ok, b, 1)
                need(pool, U_ps, b - 1, 6)
                pool.tensor_tensor(x_lo[:].rearrange("p c n -> p (c n)"), xn[:],
                                   x_hi[:].rearrange("p c n -> p (c n)").bitcast(F32), ALU.subtract).then_inc(xlo_ok.sem, 1)

            def split_piece(e, p):
                s, k = p % 2, p // 2
                need(pool, eraw_ld[s], e, 32 * (k + 1))
                need(pool, epart_st[s], e, 32 * k)
                pool.sem_inc(pool_turn, 1)
                pool.tensor_copy(e_hi[:, s, :], e_raw[:, s, :]).then_inc(ehi_ok.sem, 1)
                need(pool, ehi_ok, e, p + 1)
                pool.tensor_tensor(e_raw[:, s, :], e_raw[:, s, :], e_hi[:, s, :].bitcast(F32), ALU.subtract).then_inc(elo_ok.sem, 1)

            pool.memset(tri[:].bitcast(F32), 1.0).then_inc(pool_turn, 1)
            pool.memset(eye[:], 0.0).then_inc(pool_turn, 1)
            pool.wait_ge(pool_turn, 2)
            pool.affine_select(out=eye[:], in_=eye[:], compare_op=ALU.not_equal, fill=1.0, base=0,
                               pattern=[[-1, P]], channel_multiplier=1).then_inc(consts, 1)
            pool.affine_select(out=tri[:], in_=tri[:].bitcast(F32), compare_op=ALU.is_gt, fill=0.0, base=0,
                               pattern=[[1, P]], channel_multiplier=-1).then_inc(consts, 1)
            pool.iota(iota[:], pattern=[[1, P]], base=0, channel_multiplier=0,
                      allow_small_or_imprecise_dtypes=True)
            pool.iota(spare_row[:], pattern=[[0, 1]], base=TOK, channel_multiplier=1,
                      allow_small_or_imprecise_dtypes=True).then_inc(consts, 1)
            pool.iota(tab[:, 0, :], pattern=[[0, P]], base=TOK, channel_multiplier=1,
                      allow_small_or_imprecise_dtypes=True)
            pool.iota(tok_c[:], pattern=[[P, T]], base=-TOK, channel_multiplier=1,
                      allow_small_or_imprecise_dtypes=True).then_inc(consts, 1)
            x_lo_part(0)
            for u in range(4):
                square_unit(0, u)
            x_lo_part(1)

            def step(b, nxt, ahead):
                n = b + 1
                for p in range(3):
                    split_piece(b, p)
                for u in range(4):
                    if nxt:
                        square_unit(n, u)
                    if u < 3:
                        split_piece(b, 3 + u)
                if ahead:
                    x_lo_part(b + 2)

            step(0, True, True)
            with pool.Fori(1, B - 2) as b:
                step(b, True, True)
            step(B - 2, True, False)
            step(B - 1, False, False)

            def column(k):
                return pool.value_load(sched[0:1, 0, ds(k, 1)], min_val=0, max_val=P)

            def gather(k, s):
                col = column(k)
                need(pool, xg_ld[s], k - 2, 16 - 8 * s)
                pool.sem_inc(pool_turn, 1)
                pool.tensor_copy(g_idx[:, s, :], tab_id[:, ds(col, 1)]).then_inc(col_ok.sem, 1)
                need(pool, xgT_ps, k - 2, 1)
                pool.sem_inc(pool_turn, 1)
                need(pool, col_ok, k, 1)
                pool.sem_inc(pool_turn, 1)
                pool.indirect_dma_start(out=xg[:, s, :], out_offset=None, in_=h_rows,
                                        in_offset=bass.IndirectOffsetOnAxis(ap=g_idx[:, s, :].bitcast(U32), axis=0)).then_inc(xg_ld[s].sem, 16)

            def pick(k, s):
                col = column(k)
                need(pool, y_ok, k - 2, 1)
                pool.sem_inc(pool_turn, 1)
                need(pool, acc_st, k - 2, 16)
                pool.sem_inc(pool_turn, 1)
                pool.tensor_copy(w_sel[:, s, :], tab_w[:, ds(col, 1)]).then_inc(wsel_ok.sem, 1)
                pool.tensor_copy(s_idx[:, s, :], tab_id[:, ds(col, 1)]).then_inc(wsel_ok.sem, 1)

            def scatter(k, s):
                need(pool, acc_st, k - 1, 16)
                pool.sem_inc(pool_turn, 1)
                need(pool, wsel_ok, k, 2)
                pool.sem_inc(pool_turn, 1)
                need(pool, y_ok, k, 1)
                pool.sem_inc(pool_turn, 1)
                pool.indirect_dma_start(out=out, out_offset=bass.IndirectOffsetOnAxis(ap=s_idx[:, s, :].bitcast(U32), axis=0),
                                        in_=y_sb[:, s, :], in_offset=None, compute_op=ALU.add).then_inc(acc_st.sem, 16)

            pool.wait_ge(spare_st, 32)
            for t in range(T):
                need(pool, row_st[t], B - 1, 32)
            pool.wait_ge(sched_ok, 1)
            pool.wait_ge(tabs_ok, 1)

            def blk_stage(k, par):
                if not isinstance(k, int) or k + 4 < MAX_BLOCKS:
                    gather(k + 4, par)
                if not isinstance(k, int) or 0 <= k < MAX_BLOCKS:
                    pick(k, par)
                if not isinstance(k, int) or 0 <= k - 1:
                    scatter(k - 1, (par + 1) % 2)

            for k in range(-4, 3):
                blk_stage(k, k % 2)
            pairs = (MAX_BLOCKS - 3 - 4) // 2
            with pool.Fori(0, pairs) as j:
                blk_stage(2 * j + 3, 1)
                blk_stage(2 * j + 4, 0)
            for k in range(3 + 2 * pairs, MAX_BLOCKS + 1):
                blk_stage(k, k % 2)


_INS = ['x', 'cond_2048', 'L0_cond_W_emb', 'L0_cond_b_emb', 'L0_cond_g_norm', 'L0_cond_W_qkv', 'L0_cond_g_q',
        'L0_cond_g_k', 'L0_cond_W_out', 'L0_ffn_W_gate', 'L0_ffn_w_gate_proj', 'L0_ffn_w_up_proj', 'L0_ffn_w_down_proj']


def kernel(**inputs):
    import numpy as np
    import concourse.bacc as bacc
    from concourse.bass_utils import run_bass_kernel_spmd

    nc = bacc.Bacc("TRN2", target_bir_lowering=False, num_devices=1)
    arrays, args = {}, []
    for name in _INS:
        a = np.ascontiguousarray(inputs[name])
        arrays[f"in_{name}"] = a
        args.append(nc.dram_tensor(f"in_{name}", a.shape, mybir.dt.from_np(a.dtype), kind="ExternalInput").ap())
    b, n, d = inputs["x"].shape
    out = nc.dram_tensor("out_rows", (b * n + P, d), F32, kind="ExternalOutput").ap()
    adaln_moe_kernel(nc, *args, out)
    r = run_bass_kernel_spmd(nc, [arrays], core_ids=[0])
    return r.results[0]["out_rows"][:b * n].reshape(b, n, d)
```

```python
from contextlib import ExitStack

import concourse.bass as bass
from concourse import mybir

ALU = mybir.AluOpType
ACT = mybir.ActivationFunctionType
AX = mybir.AxisListType
F32 = mybir.dt.float32
F32R = mybir.dt.float32r
I32 = mybir.dt.int32
U32 = mybir.dt.uint32
ds = bass.ds

P = 128
EPS = 1e-6
TOP_K = 2
SOFTMAX_SAFE = 80.0
RSQRT_MAGIC = float(0x5F3759DF)


class Signal:

    def __init__(self, sem, per, start=0):
        self.sem, self.per, self.start = sem, per, start

    def at(self, b, k):
        return b * self.per + k + self.start


def need(eng, signal, b, k):
    value = signal.at(b, k)
    if isinstance(value, int) and value <= signal.start:
        return
    eng.wait_ge(signal.sem, value)


class Chain:

    def __init__(self, eng, sem, per):
        self.eng = eng
        self.begin(sem, per)

    def begin(self, sem, per):
        self.sem, self.per, self.base, self.n = sem, per, 0, 0

    def open(self, b):
        self.base, self.n = b * self.per, 0

    def link(self, ins):
        ins.then_inc(self.sem, 1)
        self.n += 1

    def settle(self):
        self.eng.wait_ge(self.sem, self.base + self.n)

    def close(self):
        assert self.n <= self.per, (self.n, self.per)
        if self.n < self.per:
            if self.n or not isinstance(self.base, int) or self.base:
                self.settle()
            self.eng.sem_inc(self.sem, self.per - self.n)


def bcast(ap, axis, n):
    dims = [list(x) for x in ap.ap]
    dims.insert(axis, [0, n])
    return bass.AP(ap.tensor, ap.offset, dims)


def adaln_moe_kernel(nc, x, cond, w_emb, b_emb, g_norm, w_qkv, g_q, g_k, w_out,
                     w_gate, w_gp, w_up, w_dn, out):
    B, N, D = x.shape
    E, _, H = w_gp.shape
    DH = g_q.shape[0]
    HEADS = D // DH
    T = N // P
    C = D // P
    TOK = B * N
    G = HEADS // 4
    HC = H // P
    PIECES = C + HC
    WOC = D + E
    HALF = WOC // 2
    BPE = TOK // P
    MAX_BLOCKS = (TOP_K * TOK - E) // P + E
    PARTS = 3 * DH
    NSLOT = 5
    assert (T, C, G, HC, D, 2 * H, DH, E) == (2, 4, 4, 2, 512, 512, 32, 8)

    h_rows = nc.dram_tensor("h_rows", (TOK + P, D), F32).ap()
    w_parts = nc.dram_tensor("w_parts", (E, P, 2, PIECES, D), F32).ap()

    ctx = ExitStack()
    with ctx:
        def sb(name, shape, dt=F32, stack=ctx):
            return stack.enter_context(nc.sbuf_tensor(name, [P, *shape], dt))

        def sem(name):
            return ctx.enter_context(nc.semaphore(name))

        ps_p = ctx.enter_context(nc.psum_tensor("ps_p", [P, 2, 512], F32))
        ps_t = ctx.enter_context(nc.psum_tensor("ps_t", [P, 2, 512], F32))
        ps_s = ctx.enter_context(nc.psum_tensor("ps_s", [P, 2, 512], F32))
        ps_v = ctx.enter_context(nc.psum_tensor("ps_v", [P, 2, 512], F32))

        ident_r = sb("ident_r", [P], F32R)
        ident = ident_r[:].bitcast(F32)
        iota = sb("iota", [P])
        tab = sb("tab", [3, P])
        base = sb("base", [E])
        tab_id = sb("tab_id", [P + 1], I32)
        tab_w = sb("tab_w", [P + 1])
        spare_row = sb("spare_row", [1])
        sched = sb("sched", [3, MAX_BLOCKS], I32)
        free_at = sb("free_at", [E], I32)
        n_i = sb("n_i", [E], I32)

        pa = ExitStack()
        A = lambda name, shape, dt=F32: sb(name, shape, dt, pa)
        wq_hi = A("wq_hi", [C, 3 * D], F32R)
        wq_lo = A("wq_lo", [C, 3 * D], F32R)
        wo_hi = A("wo_hi", [C, WOC], F32R)
        wo_lo = A("wo_lo", [C, WOC], F32R)
        stage = A("stage", [12 * 512])
        probs = stage[:, 0:4096].rearrange("p (r n) -> p r n", r=8)
        qk_raw = stage[:, 4096:6144].rearrange("p (u n) -> p u n", u=4)
        wq_raw = stage[:, :].rearrange("p (c n) -> p c n", c=C)
        tmp = ExitStack()
        wemb = sb("wemb", [C, 2 * D], F32, tmp)
        emb = sb("emb", [D], F32, tmp)
        vecs = sb("vecs", [P], F32, tmp)
        wgate = sb("wgate", [D], F32, tmp)
        g_row = sb("g_row", [3, DH], F32, tmp)
        eye = sb("eye", [P], F32, tmp)
        sb("unused", [(2 * T * HEADS * PARTS) - (C * 2 * D + 2 * D + 2 * P + 3 * DH)], F32, tmp)
        wpr = sb("wpr", [C, WOC], F32, tmp)
        woutT = sb("woutT", [C, D], F32, tmp)
        mod_sb = sb("mod_sb", [2, D], F32, tmp)
        wc_sb = sb("wc_sb", [D], F32, tmp)
        tmp.close()
        q_cat, k_cat = zip(*[(A(f"q_cat{s}", [T, HEADS, PARTS], F32R), A(f"k_cat{s}", [T, HEADS, PARTS], F32R)) for s in range(2)])
        x_in = A("x_in", [T, D])
        xn = A("xn", [T * D])
        xr_v = xn[:, :].rearrange("p (t d) -> p t d", t=T)
        xn_v = xn[:, :].rearrange("p (c n) -> p c n", c=C)
        x_hi = A("x_hi", [C, N], F32R)
        x_lo = A("x_lo", [C, N], F32R)
        sq = A("sq", [2, D])
        work = sq[:].rearrange("p a n -> p (a n)")
        sched_ge = work[:, 0:MAX_BLOCKS * E].rearrange("p (b e) -> p b e", e=E)
        sched_t = work[:, 512:512 + 4 * MAX_BLOCKS].rearrange("p (a b) -> p a b", a=4)
        sched_f = work[:, 768:768 + 4 * E].rearrange("p (a e) -> p a e", a=4)
        v_sb = A("v_sb", [T, D])
        stk = A("stk", [4, 512], F32R)
        o_f = A("o_f", [2, N])
        o_hi = A("o_hi", [G, N], F32R)
        o_lo = A("o_lo", [G, N], F32R)
        h_sb = A("h_sb", [T, WOC])
        xres = A("xres", [T, D])
        tri = A("tri", [P], F32R)
        ones_r = A("ones_r", [P], F32R)
        ones_f = ones_r[:].bitcast(F32)
        gains = A("gains", [DH])
        a_mod = A("a_mod", [C, B])
        s_mod = A("s_mod", [C, B])
        embT = A("embT", [C, B])
        vecT = A("vecT", [12])
        wgT = A("wgT", [C, E])
        g_max = A("g_max", [2])
        shift = A("shift", [1])
        st_x = A("st_x", [5, T])
        st_q = A("st_q", [2, 4, 2 * HEADS])
        st_s = A("st_s", [2, 2 * HEADS])
        top_v = A("top_v", [T, 8])
        top_i = A("top_i", [T, 8], U32)
        top_f = A("top_f", [T, 2])
        oh = A("oh", [2, T, E])
        ohr = A("ohr", [2, T, E])
        mask = A("mask", [T, E], F32R)
        ranks = A("ranks", [T, E])
        rt = A("rt", [12, 2, T])
        rt_i = A("rt_i", [3, 2, T], I32)
        w_hi_r = A("w_hi_r", [2, T], F32R)
        tok_c = A("tok_c", [T])
        one_r = A("one_r", [2, P], F32R)
        one_c = A("one_c", [2, 3, P], F32R)
        e_raw = A("e_raw", [2, D])
        e_hi = A("e_hi", [2, D], F32R)
        pa.close()

        pb = ExitStack()
        Bt = lambda name, shape, dt=F32: sb(name, shape, dt, pb)
        w_sl = Bt("w_sl", [NSLOT, 2, PIECES, D], F32R)
        xg = Bt("xg", [2, D])
        xg_hi = Bt("xg_hi", [2, D], F32R)
        xg_lo = Bt("xg_lo", [2, D], F32R)
        sg = Bt("sg", [2, H])
        gu = Bt("gu", [2, H])
        gu_hi = Bt("gu_hi", [2, H], F32R)
        gu_lo = Bt("gu_lo", [2, H], F32R)
        y_sb = Bt("y_sb", [2, D])
        g_idx = Bt("g_idx", [2, 1], I32)
        s_idx = Bt("s_idx", [2, 1], I32)
        w_sel = Bt("w_sel", [2, 1])
        pb.close()

        ld_emb, ld_vecs, ld_gains, ld_wout, ld_wgate = (sem(n) for n in ("ld_emb", "ld_vecs", "ld_gains", "ld_wout", "ld_wgate"))
        ld_wemb = [sem(f"ld_wemb{i}") for i in range(2)]
        ld_wq = [sem(f"ld_wq{c}") for c in range(C)]
        consts, zeroed, spare_st = sem("consts"), sem("zeroed"), sem("spare_st")
        small_T, small_ok = sem("small_T"), sem("small_ok")
        mod_ps, mod_rows, mod_T = sem("mod_ps"), sem("mod_rows"), sem("mod_T")
        mod_ok = sem("mod_ok")
        gains_raw, gains_ps, gains_ok = sem("gains_raw"), sem("gains_ps"), sem("gains_ok")
        diag_ok, wT_ps, wT_ok = sem("diag_ok"), sem("wT_ps"), sem("wT_ok")
        wc_ps, wc_rows, wc_T, wpr_ok = sem("wc_ps"), sem("wc_rows"), sem("wc_T"), sem("wpr_ok")
        wqhi_ok, wqlo_ok, wqlo0_ok = sem("wqhi_ok"), sem("wqlo_ok"), sem("wqlo0_ok")
        wohi_ok, wolo_ok = sem("wohi_ok"), sem("wolo_ok")
        setup_step = sem("setup_step")
        sp_turn, pool_turn, dve_turn = sem("sp_turn"), sem("pool_turn"), sem("dve_turn")

        sig = lambda name, per: Signal(sem(name), per)
        x_ld, xres_ld = sig("x_ld", 16), sig("xres_ld", 16)
        row_st = [sig(f"row_st{t}", 32) for t in range(T)]
        eraw_ld = [sig(f"eraw_ld{s}", 16 * PIECES) for s in range(2)]
        epart_st = [sig(f"epart_st{s}", 16 * PIECES) for s in range(2)]
        x_sq = sig("x_sq", T)
        xr_ok = sig("xr_ok", T)
        xT_ps = sig("xT_ps", 1)
        xn_ok = sig("xn_ok", C)
        xhi_ok = sig("xhi_ok", 1)
        xlo_ok = sig("xlo_ok", 1)
        U_ps = sig("U_ps", 6)
        U_ev = sig("U_ev", 6)
        qk_sq = sig("qk_sq", 4)
        gain_ok = sig("gain_ok", 2)
        hs_ok = sig("hs_ok", 4)
        qk_n = sig("qk_n", 4)
        qk_hi = sig("qk_hi", 4)
        qk_lo = sig("qk_lo", 4)
        T_ps = sig("T_ps", HEADS)
        T_ea, T_ed = sig("T_ea", HEADS // 2), sig("T_ed", HEADS // 2)
        S_ps = sig("S_ps", HEADS)
        ex_ok = sig("ex_ok", HEADS)
        V_ps = sig("V_ps", G)
        nrm = sig("nrm", G)
        ohi_ok, olo_ok = sig("ohi_ok", G), sig("olo_ok", G)
        H_ps = sig("H_ps", T)
        H_ev = sig("H_ev", T)
        xh_ok = sig("xh_ok", T)
        ed_ok = sig("ed_ok", 1)
        dif_ok = sig("dif_ok", 1)
        mask_ok = sig("mask_ok", 1)
        Rp_ps = sig("Rp_ps", 1)
        rank_ev = Signal(sem("rank_ev"), 1, start=1)
        hot_ok = sig("hot_ok", 4)
        Rt_ps = sig("Rt_ps", 4)
        tab_ev = Signal(sem("tab_ev"), 1, start=1)
        ehi_ok, elo_ok = sig("ehi_ok", PIECES), sig("elo_ok", PIECES)
        dve_step = sem("dve_step")
        DVE_STEPS = 80

        sched_ok, tabs_ok = sem("sched_ok"), sem("tabs_ok")
        w_ld = sem("w_ld")
        blk = lambda name, per=1: sig(name, per)
        col_ok = blk("col_ok", 1)
        xg_ld = [blk(f"xg_ld{s}", 8) for s in range(2)]
        xgT_ps, xgh_ok, xgl_ok = blk("xgT_ps"), blk("xgh_ok"), blk("xgl_ok")
        gu_ps = blk("gu_ps")
        e_ok = blk("e_ok")
        gu_ok = blk("gu_ok")
        gT_ps, gh_ok, gl_ok = blk("gT_ps"), blk("gh_ok"), blk("gl_ok")
        y_ps = Signal(sem("y_ps"), 1, start=1)
        wsel_ok = blk("wsel_ok", 2)
        y_ok = blk("y_ok")
        acc_st = blk("acc_st", 16)
        blk_step = sem("blk_step")

        U_TILE = [0, 0, 1, 1, 0, 1]
        U_KIND = [0, 1, 0, 1, 2, 2]
        U_BANK = [0, 1, 1, 0, 0, 1]

        block = ctx.enter_context(nc.Block())

        @block.sync
        def _(sp):
            def rows(t, b):
                return x[ds(b, 1), t * P:(t + 1) * P, :].rearrange("a p d -> p (a d)")

            def load_x(b):
                need(sp, x_sq, b - 1, T)
                need(sp, xr_ok, b - 1, T)
                sp.dma_start(x_in[:], x[ds(b, 1)].rearrange("a (t p) d -> p (a t) d", p=P)).then_inc(x_ld.sem, 16)

            def load_residual(b):
                for t in range(T):
                    need(sp, row_st[t], b - 1, 32)
                sp.dma_start(xres[:], x[ds(b, 1)].rearrange("a (t p) d -> p (a t) d", p=P)).then_inc(xres_ld.sem, 16)

            def load_piece(e, p):
                s, k = p % 2, p // 2
                need(sp, epart_st[s], e, 32 * k)
                if p < C:
                    srcs = [w[ds(e, 1), p * P:(p + 1) * P, :] for w in (w_gp, w_up)]
                else:
                    m = p - C
                    srcs = [w_dn[ds(e, 1), m * P:(m + 1) * P, i * H:(i + 1) * H] for i in range(2)]
                for i, src in enumerate(srcs):
                    sp.dma_start(e_raw[:, s, i * H:(i + 1) * H], src.rearrange("a p h -> p (a h)")).then_inc(eraw_ld[s].sem, 16)

            def store_piece(e, p):
                s = p % 2
                need(sp, elo_ok, e, p + 1)
                sp.dma_start(w_parts[ds(e, 1), :, 0, p, :].rearrange("a p d -> p (a d)"), e_hi[:, s, :].bitcast(F32)).then_inc(epart_st[s].sem, 16)
                sp.dma_start(w_parts[ds(e, 1), :, 1, p, :].rearrange("a p d -> p (a d)"), e_raw[:, s, :]).then_inc(epart_st[s].sem, 16)

            sp.dma_start(emb[0:B, :], cond).then_inc(ld_emb, 16)
            load_x(0)
            sp.dma_start(vecs[0:8, :], b_emb.rearrange("(a p) -> a p", p=P)).then_inc(ld_vecs, 16)
            sp.dma_start(vecs[8:12, :], g_norm.rearrange("(a p) -> a p", p=P)).then_inc(ld_vecs, 16)
            sp.dma_start(wgate[0:E, :], w_gate).then_inc(ld_wgate, 16)
            for i in range(2):
                sp.dma_start(wemb[:, :, i * D:(i + 1) * D], w_emb[:, i * D:(i + 1) * D].rearrange("(c p) n -> p c n", p=P)).then_inc(ld_wemb[i], 16)
            sp.dma_start(g_row[0:1, 0, :], g_q.rearrange("(a d) -> a d", a=1)).then_inc(ld_gains, 16)
            sp.dma_start(g_row[0:1, 1, :], g_k.rearrange("(a d) -> a d", a=1)).then_inc(ld_gains, 16)
            sp.dma_start(wpr[:, :, 0:D], w_out.rearrange("(c p) n -> p c n", p=P)).then_inc(ld_wout, 16)
            for c in range(C):
                sp.dma_start(wq_raw[:, c, :], w_qkv[c * P:(c + 1) * P, :]).then_inc(ld_wq[c], 16)
            sp.wait_ge(zeroed, 1)
            sp.dma_start(h_rows[TOK:TOK + P], xres[:, 0, :]).then_inc(spare_st, 16)
            sp.dma_start(out[TOK:TOK + P], xres[:, 0, :]).then_inc(spare_st, 16)
            load_x(1)
            sp.wait_ge(spare_st, 32)

            def step(b, ahead, more=True):
                load_residual(b)
                for p in range(PIECES):
                    store_piece(b, p)
                    if ahead and p == 1:
                        load_x(b + 3)
                    if p + 2 < PIECES:
                        load_piece(b, p + 2)
                    elif more:
                        load_piece(b + 1, p + 2 - PIECES)
                for t in range(T):
                    r = ds(b * N + t * P, P)
                    need(sp, H_ev, b, t + 1)
                    sp.dma_start(h_rows[r], h_sb[:, t, 0:D]).then_inc(row_st[t].sem, 16)
                    need(sp, xh_ok, b, t + 1)
                    sp.dma_start(out[r], xres[:, t, :]).then_inc(row_st[t].sem, 16)
                sp.sem_inc(sp_turn, 1)

            load_piece(0, 0)
            load_piece(0, 1)
            load_x(2)
            step(0, True)
            with sp.Fori(1, B - 3) as b:
                step(b, True)
            step(B - 3, False)
            step(B - 2, False)
            step(B - 1, False, False)

            def load_expert(e):
                if e < NSLOT:
                    if e == 0:
                        need(sp, U_ps, B - 1, 6)
                        for s in range(2):
                            need(sp, epart_st[s], B - 1, 16 * PIECES)
                    if e == 2:
                        sp.wait_ge(tabs_ok, 1)
                        for t in range(T):
                            need(sp, row_st[t], B - 1, 32)
                else:
                    last = sp.value_load(free_at[0:1, e - NSLOT:e - NSLOT + 1], min_val=1, max_val=MAX_BLOCKS + 1)
                    sp.wait_ge(y_ps.sem, last)
                sp.dma_start(w_sl[:, e % NSLOT].bitcast(F32), w_parts[e]).then_inc(w_ld, 16)
                sp.wait_ge(w_ld, 16 * (e + 1))

            for e in range(E):
                load_expert(e)
            need(sp, acc_st, MAX_BLOCKS - 1, 16)

        @block.tensor
        def _(pe):
            def split_mm(o, l_hi, l_lo, r_hi, r_lo, first, last):
                pe.matmul(o, l_hi, r_hi, start=first, stop=False)
                pe.matmul(o, l_lo, r_hi, start=False, stop=False)
                return pe.matmul(o, l_hi, r_lo, start=False, stop=last)

            def transpose_x(b):
                need(pe, xr_ok, b, T)
                for c in range(C):
                    for t in range(T):
                        o = (c % 2) * N + t * P
                        last = pe.transpose(ps_t[:, c // 2, o:o + P], xr_v[:, t, c * P:(c + 1) * P], ident)
                last.then_inc(xT_ps.sem, 1)

            def unit_part(b, u, c):
                t, kind = U_TILE[u], U_KIND[u]
                if c == 0 and u == 0:
                    need(pe, xhi_ok, b, 1)
                    need(pe, xlo_ok, b, 1)
                o = ps_p[:, U_BANK[u], :]
                r = slice(t * P, (t + 1) * P)
                n = slice(kind * D, (kind + 1) * D)
                last = split_mm(o, x_hi[:, c, r], x_lo[:, c, r], wq_hi[:, c, n], wq_lo[:, c, n],
                                c == 0, c == C - 1)
                if c == C - 1:
                    last.then_inc(U_ps.sem, 1)

            def stack(b, s, h):
                if h == 0:
                    need(pe, qk_hi, b, 4)
                    need(pe, qk_lo, b, 4)
                if h >= 2:
                    need(pe, T_ea if h % 2 == 0 else T_ed, b, h // 2)
                for i, cat in enumerate((q_cat[s], k_cat[s])):
                    for t in range(T):
                        o = i * N + t * P
                        last = pe.transpose(ps_t[0:PARTS, h % 2, o:o + P].bitcast(F32R), cat[:, t, h, :], ident_r[:])
                last.then_inc(T_ps.sem, 1)

            def scores(b, h):
                need(pe, T_ea if h % 2 == 0 else T_ed, b, h // 2 + 1)
                need(pe, ex_ok, b, h - 1)
                k = stk[0:PARTS, h % 4, :]
                for i in range(T):
                    last = pe.matmul(ps_s[:, h % 2, i * N:(i + 1) * N], k[:, N + i * P:N + (i + 1) * P],
                                     k[:, 0:N], start=True, stop=True)
                last.then_inc(S_ps.sem, 1)

            def values(b, g, step):
                if step == 0:
                    need(pe, ex_ok, b, 4 * g + 4)
                    need(pe, U_ev, b, 6)
                    need(pe, nrm, b, g - 1)
                    need(pe, H_ev, b - 1, T)
                i = step % 2
                for j in range(4):
                    h = 4 * g + j
                    q = slice(32 * j, 32 * j + 32)
                    lhs = v_sb[:, i, h * DH:(h + 1) * DH] if step < 2 else ones_f[:, 0:DH]
                    o = (step // 2) * N
                    last = pe.matmul(ps_v[q, g % 2, o:o + N], lhs, probs[:, h % 8, i * N:(i + 1) * N],
                                     start=(i == 0), stop=(i == 1))
                if step == 3:
                    last.then_inc(V_ps.sem, 1)

            def out_proj(b, t):
                r = slice(t * P, (t + 1) * P)
                ps_h = (ps_p, ps_v)[t]
                need(pe, ohi_ok, b, G)
                need(pe, olo_ok, b, G)
                for c in range(C):
                    for i in range(2):
                        n = slice(i * HALF, (i + 1) * HALF)
                        last = split_mm(ps_h[:, i, 0:HALF], o_hi[:, c, r], o_lo[:, c, r],
                                        wo_hi[:, c, n], wo_lo[:, c, n], c == 0, c == C - 1)
                last.then_inc(H_ps.sem, 1)

            def rank_sums(b):
                need(pe, mask_ok, b, 1)
                o = ps_v[:, 1, :]
                pe.matmul(o[:, 0:E], tri[:], mask[:, 0, :], start=True, stop=True)
                pe.matmul(o[:, E:2 * E], tri[:], mask[:, 1, :], start=True, stop=False)
                pe.matmul(o[:, E:2 * E], ones_r[:], mask[:, 0, :], start=False, stop=True)
                pe.matmul(o[:, 2 * E:3 * E], ones_r[:], mask[:, 0, :], start=True, stop=False)
                pe.matmul(o[:, 2 * E:3 * E], ones_r[:], mask[:, 1, :], start=False, stop=True).then_inc(Rp_ps.sem, 1)

            def table_sums(b, i0):
                for i in range(i0, i0 + 2):
                    need(pe, hot_ok, b, i + 1)
                    pe.matmul(ps_p[:, 0, 0:3 * P], one_r[:, i % 2, :], one_c[:, i % 2].rearrange("p a n -> p (a n)"),
                              start=(i == 0), stop=(i == 3)).then_inc(Rt_ps.sem, 1)

            pe.wait_ge(consts, 6)
            pe.wait_ge(ld_emb, 16)
            for c in range(C):
                pe.transpose(ps_p[:, 0, c * B:(c + 1) * B], emb[0:B, c * P:(c + 1) * P], ident[0:B, 0:B])
            pe.wait_ge(ld_vecs, 32)
            pe.transpose(ps_p[:, 0, 64:76], vecs[0:12, :], ident[0:12, 0:12])
            pe.wait_ge(ld_wgate, 16)
            for c in range(C):
                last = pe.transpose(ps_p[:, 0, 128 + c * E:128 + (c + 1) * E], wgate[0:E, c * P:(c + 1) * P], ident[0:E, 0:E])
            last.then_inc(small_T, 1)
            pe.wait_ge(small_ok, 1)
            for i in range(2):
                pe.wait_ge(ld_wemb[i], 16)
                for k in range(C):
                    last = pe.matmul(ps_v[0:B, i, :], embT[:, k, :], wemb[:, k, i * D:(i + 1) * D],
                                     start=(k == 0), stop=(k == C - 1))
            last.then_inc(mod_ps, 1)
            transpose_x(0)
            pe.wait_ge(mod_rows, 1)
            for i in range(2):
                for c in range(C):
                    n = i * C + c
                    last = pe.transpose(ps_p[:, 0, n * B:(n + 1) * B], mod_sb[0:B, i, c * P:(c + 1) * P], ident[0:B, 0:B])
            last.then_inc(mod_T, 1)
            pe.wait_ge(gains_raw, 1)
            pe.matmul(ps_s[:, 0, 0:DH], ones_f[0:1, :], g_row[0:1, 2, :], start=True, stop=True).then_inc(gains_ps, 1)
            pe.wait_ge(diag_ok, 1)
            for n in range(C):
                if n >= 2:
                    pe.wait_ge(wT_ok, n - 1)
                for m in range(C):
                    bank = (ps_s, ps_p)[n % 2]
                    last = pe.transpose(bank[:, 1, m * P:(m + 1) * P], wpr[:, m, n * P:(n + 1) * P], ident)
                last.then_inc(wT_ps, 1)
            for n in range(C):
                pe.wait_ge(wT_ok, n + 1)
                last = pe.matmul(ps_v[0:E, 0, :], wgT[:, n, :], woutT[:, n, :], start=(n == 0), stop=(n == C - 1))
            last.then_inc(wc_ps, 1)

            pe.wait_ge(mod_ok, 1)
            pe.wait_ge(wqhi_ok, C)
            pe.wait_ge(wqlo_ok, C - 1)
            pe.wait_ge(wqlo0_ok, 1)
            for u in range(6):
                if u >= 2:
                    need(pe, U_ev, 0, [0, 0, 2, 1, 4, 3][u])
                for c in range(C):
                    unit_part(0, u, c)
                if u == 1:
                    pe.wait_ge(wc_rows, 1)
                    for c in range(C):
                        last = pe.transpose(ps_v[:, 1, c * E:(c + 1) * E], wc_sb[0:E, c * P:(c + 1) * P], ident[0:E, 0:E])
                    last.then_inc(wc_T, 1)
            need(pe, xn_ok, 0, C)
            transpose_x(1)

            def step(b, s, nxt, ahead, routed):
                n = b + 1
                if nxt:
                    need(pe, xn_ok, n, C // 2)
                else:
                    need(pe, T_ea, b - 1, 8)
                    need(pe, T_ed, b - 1, 8)
                stack(b, s, 0)
                if nxt:
                    need(pe, xn_ok, n, C)
                stack(b, s, 1)
                for g in range(G):
                    for j in range(4):
                        h = 4 * g + j
                        scores(b, h)
                        if h + 2 < HEADS:
                            stack(b, s, h + 2)
                        if nxt:
                            if j == 0:
                                if g == 0 or g == 1:
                                    need(pe, H_ev, b - 1, T)
                                elif g == 2:
                                    need(pe, U_ev, n, 2)
                                elif routed:
                                    need(pe, tab_ev, b - 1, 1)
                                else:
                                    need(pe, U_ev, n, 1)
                            unit_part(n, g, j)
                        if g >= 1:
                            if g == 2 and j == 0 and routed:
                                need(pe, rank_ev, b - 1, 1)
                            values(b, g - 1, j)
                        if routed and (g, j) == (0, 3):
                            need(pe, H_ev, b - 1, T)
                            rank_sums(b - 1)
                        if routed and (g, j) == (2, 0):
                            if nxt:
                                need(pe, U_ev, n, 1)
                            table_sums(b - 1, 0)
                        if routed and (g, j) == (2, 2):
                            table_sums(b - 1, 2)
                for j in range(4):
                    values(b, G - 1, j)
                if nxt:
                    need(pe, U_ev, n, 4)
                    for c in range(C):
                        unit_part(n, 4, c)
                    need(pe, U_ev, n, 3)
                    for c in range(C):
                        unit_part(n, 5, c)
                if ahead:
                    need(pe, T_ea, b, 8)
                    need(pe, T_ed, b, 8)
                    transpose_x(b + 2)
                if nxt:
                    need(pe, U_ev, n, 6)
                else:
                    need(pe, tab_ev, b - 1, 1)
                if isinstance(b, int) and b == 0:
                    pe.wait_ge(wohi_ok, 2)
                    pe.wait_ge(wolo_ok, 1)
                for t in range(T):
                    out_proj(b, t)

            step(0, 0, True, True, False)
            with pe.Fori(0, (B - 2) // 2 - 1) as j:
                step(2 * j + 1, 1, True, True, True)
                step(2 * j + 2, 0, True, True, True)
            step(B - 3, 1, True, True, True)
            step(B - 2, 0, True, False, True)
            step(B - 1, 1, False, False, True)
            need(pe, H_ev, B - 1, T)
            rank_sums(B - 1)
            table_sums(B - 1, 0)
            table_sums(B - 1, 2)

            pe.sem_inc(y_ps.sem, 1)
            pe.wait_ge(sched_ok, 1)

            def rows_T(k, s):
                need(pe, xg_ld[s], k, 16 - 8 * s)
                need(pe, xgl_ok, k - 2, 1)
                for c in range(C):
                    last = pe.transpose(ps_t[:, s, c * P:(c + 1) * P], xg[:, s, c * P:(c + 1) * P], ident)
                last.then_inc(xgT_ps.sem, 1)

            def slot_of(k):
                return pe.value_load(sched[0:1, 1, ds(k, 1)], min_val=0, max_val=NSLOT - 1)

            def gate_up(k, s):
                e = pe.value_load(sched[0:1, 2, ds(k, 1)], min_val=16, max_val=16 * E)
                w = slot_of(k)
                pe.wait_ge(w_ld, e)
                need(pe, xgh_ok, k, 1)
                need(pe, xgl_ok, k, 1)
                need(pe, gu_ok, k - 2, 1)
                o = ps_p[:, s, :]
                for c in range(C):
                    n = slice(c * P, (c + 1) * P)
                    hi = w_sl[:, ds(w, 1), 0, c, :].rearrange("p a n -> p (a n)")
                    lo = w_sl[:, ds(w, 1), 1, c, :].rearrange("p a n -> p (a n)")
                    last = split_mm(o, xg_hi[:, s, n], xg_lo[:, s, n], hi, lo, c == 0, c == C - 1)
                last.then_inc(gu_ps.sem, 1)

            def act_T(k, s):
                need(pe, gu_ok, k, 1)
                need(pe, gl_ok, k - 2, 1)
                for c in range(HC):
                    last = pe.transpose(ps_v[:, s, c * P:(c + 1) * P], gu[:, s, c * P:(c + 1) * P], ident)
                last.then_inc(gT_ps.sem, 1)

            def down(k, s):
                w = slot_of(k)
                need(pe, gh_ok, k, 1)
                need(pe, gl_ok, k, 1)
                need(pe, y_ok, k - 2, 1)
                o = ps_s[:, s, :]
                for c in range(HC):
                    n = slice(c * P, (c + 1) * P)
                    hi = w_sl[:, ds(w, 1), 0, C + c, :].rearrange("p a n -> p (a n)")
                    lo = w_sl[:, ds(w, 1), 1, C + c, :].rearrange("p a n -> p (a n)")
                    last = split_mm(o, gu_hi[:, s, n], gu_lo[:, s, n], hi, lo, c == 0, c == HC - 1)
                last.then_inc(y_ps.sem, 1)

            def blk_stage(k, par, lo=0, hi=MAX_BLOCKS):
                if not isinstance(k, int) or k + 1 < MAX_BLOCKS and k + 1 >= 0:
                    gate_up(k + 1, (par + 1) % 2)
                if not isinstance(k, int) or 0 <= k < MAX_BLOCKS:
                    act_T(k, par)
                if not isinstance(k, int) or k + 3 < MAX_BLOCKS:
                    rows_T(k + 3, (par + 1) % 2)
                if not isinstance(k, int) or 0 <= k - 1:
                    down(k - 1, (par + 1) % 2)

            for k in range(-3, 3):
                blk_stage(k, k % 2)
            pairs = (MAX_BLOCKS - 3 - 3) // 2
            with pe.Fori(0, pairs) as j:
                blk_stage(2 * j + 3, 1)
                blk_stage(2 * j + 4, 0)
            for k in range(3 + 2 * pairs, MAX_BLOCKS + 1):
                blk_stage(k, k % 2)

        @block.scalar
        def _(act):
            def unit_out(b, u):
                need(act, U_ps, b, u + 1)
                t, kind = U_TILE[u], U_KIND[u]
                if kind < 2:
                    need(act, hs_ok, b, u - 1)
                    act.activation(sq[:, u % 2, :], ps_p[:, U_BANK[u], :], ACT.Square).then_inc(qk_sq.sem, 1)
                if kind == 2:
                    need(act, V_ps, b - 1, G)
                    dst = v_sb[:, t, :]
                else:
                    need(act, qk_hi, b - 1, u + 1)
                    need(act, qk_lo, b - 1, u + 1)
                    dst = qk_raw[:, u, :]
                act.copy(dst, ps_p[:, U_BANK[u], :]).then_inc(U_ev.sem, 1)

            def parts_hi(b, s, u):
                need(act, qk_n, b, u + 1)
                need(act, T_ps, b - 2, HEADS)
                t = U_TILE[u]
                src = bcast(qk_raw[:, u, :].rearrange("p (h d) -> p h d", d=DH), 2, 2)
                if U_KIND[u] == 0:
                    dst = q_cat[s][:, t].rearrange("p h (r d) -> p h r d", d=DH)[:, :, 0:3:2, :]
                else:
                    dst = k_cat[s][:, t].rearrange("p h (r d) -> p h r d", d=DH)[:, :, 0:2, :]
                act.copy(dst, src).then_inc(qk_hi.sem, 1)

            def square_x(b):
                need(act, x_ld, b, 16)
                need(act, xhi_ok, b - 1, 1)
                need(act, xlo_ok, b - 1, 1)
                need(act, xr_ok, b - 1, T)
                for t in range(T):
                    act.activation(xr_v[:, t, :], x_in[:, t, :], ACT.Square,
                                   accum_out=st_x[:, 0, t:t + 1]).then_inc(x_sq.sem, 1)

            def x_hi_part(b):
                need(act, xn_ok, b, C)
                need(act, U_ps, b - 1, 6)
                act.copy(x_hi[:].rearrange("p c n -> p (c n)"), xn[:]).then_inc(xhi_ok.sem, 1)

            def stack_out(b, h):
                need(act, T_ps, b, h + 1)
                need(act, S_ps, b, h - 3)
                act.copy(stk[0:PARTS, h % 4, :], ps_t[0:PARTS, h % 2, :]).then_inc(T_ea.sem, 1)

            def exps(b, h):
                need(act, S_ps, b, h + 1)
                need(act, V_ps, b, h // 4 - 1)
                act.activation(probs[:, h % 8, :], ps_s[:, h % 2, :], ACT.Exp, bias=shift[:, 0:1]).then_inc(ex_ok.sem, 1)

            def out_hi(b, g):
                need(act, nrm, b, g + 1)
                need(act, H_ps, b - 1, T)
                act.copy(o_hi[:, g, :], o_f[:, g % 2, :]).then_inc(ohi_ok.sem, 1)

            def rows_out(b, t):
                need(act, H_ps, b, t + 1)
                need(act, row_st[t], b - 1, 32)
                need(act, xh_ok, b - 1, t + 1)
                need(act, dif_ok, b - 1, 1)
                ps_h = (ps_p, ps_v)[t]
                act.copy(h_sb[:, t, 0:HALF], ps_h[:, 0, 0:HALF])
                act.copy(h_sb[:, t, HALF:WOC], ps_h[:, 1, 0:HALF]).then_inc(H_ev.sem, 1)

            def pick_exp(b):
                need(act, dif_ok, b, 1)
                act.activation(rt[:, 1, 0, :], rt[:, 0, 0, :], ACT.Exp).then_inc(ed_ok.sem, 1)

            def w_out_hi(c):
                act.wait_ge(wpr_ok, 1)
                act.copy(wo_hi[:, c:c + 2, :], wpr[:, c:c + 2, :]).then_inc(wohi_ok, 1)

            def w_qkv_hi(c):
                act.wait_ge(ld_wq[c], 16)
                act.copy(wq_hi[:, c, :], wq_raw[:, c, :]).then_inc(wqhi_ok, 1)

            def w_out_T(n):
                act.wait_ge(wT_ps, n + 1)
                act.copy(woutT[:, n, :], (ps_s, ps_p)[n % 2][:, 1, :]).then_inc(wT_ok, 1)

            def split_hi(e, p):
                s, k = p % 2, p // 2
                need(act, eraw_ld[s], e, 32 * (k + 1))
                need(act, epart_st[s], e, 32 * k)
                act.copy(e_hi[:, s, :], e_raw[:, s, :]).then_inc(ehi_ok.sem, 1)

            square_x(0)
            w_qkv_hi(0)
            w_out_T(0)
            w_out_T(1)
            w_qkv_hi(1)
            w_out_T(2)
            w_out_T(3)
            w_qkv_hi(2)
            x_hi_part(0)
            w_qkv_hi(3)
            for u in range(4):
                unit_out(0, u)
            parts_hi(0, 0, 0)
            parts_hi(0, 0, 1)
            square_x(1)
            unit_out(0, 4)
            parts_hi(0, 0, 2)
            parts_hi(0, 0, 3)
            unit_out(0, 5)
            w_out_hi(0)
            w_out_hi(2)
            x_hi_part(1)

            def step(b, s, nxt, ahead, routed):
                n, sn = b + 1, 1 - s
                stack_out(b, 0)
                for g in range(G):
                    for j in range(4):
                        h = 4 * g + j
                        if h % 2 == 0 and h + 2 < HEADS:
                            stack_out(b, h + 2)
                        exps(b, h)
                        if g == 0 and j == 2 and routed:
                            pick_exp(b - 1)
                        if g >= 2 and j == 2:
                            out_hi(b, g - 2)
                        if j == 1:
                            split_hi(b, g)
                        if g == 0 and j == 1 and ahead:
                            square_x(b + 2)
                        if g == 3 and j in (1, 2) and nxt:
                            parts_hi(n, sn, j - 1)
                    if nxt:
                        unit_out(n, g)
                out_hi(b, 2)
                out_hi(b, 3)
                if nxt:
                    unit_out(n, 4)
                    unit_out(n, 5)
                split_hi(b, 4)
                if nxt:
                    parts_hi(n, sn, 2)
                    parts_hi(n, sn, 3)
                split_hi(b, 5)
                if ahead:
                    x_hi_part(b + 2)
                rows_out(b, 0)
                rows_out(b, 1)

            step(0, 0, True, True, False)
            with act.Fori(0, (B - 2) // 2 - 1) as j:
                step(2 * j + 1, 1, True, True, True)
                step(2 * j + 2, 0, True, True, True)
            step(B - 3, 1, True, True, True)
            step(B - 2, 0, True, False, True)
            step(B - 1, 1, False, False, True)
            pick_exp(B - 1)

            def rows_hi(k, s):
                need(act, xgT_ps, k, 1)
                need(act, gu_ps, k - 2, 1)
                act.copy(xg_hi[:, s, :], ps_t[:, s, :]).then_inc(xgh_ok.sem, 1)

            def gate_exp(k, s):
                need(act, gu_ps, k, 1)
                need(act, gu_ok, k - 2, 1)
                act.activation(sg[:, s, :], ps_p[:, s, 0:H], ACT.Exp, scale=-1.0).then_inc(e_ok.sem, 1)

            def act_hi(k, s):
                need(act, gT_ps, k, 1)
                need(act, y_ps, k - 2, 1)
                act.copy(gu_hi[:, s, :], ps_v[:, s, 0:H]).then_inc(gh_ok.sem, 1)

            def rows_weighted(k, s):
                need(act, y_ps, k, 1)
                need(act, wsel_ok, k, 2)
                need(act, acc_st, k - 2, 16)
                act.activation(y_sb[:, s, :], ps_s[:, s, :], ACT.Copy, scale=w_sel[:, s, :]).then_inc(y_ok.sem, 1)

            act.wait_ge(tabs_ok, 1)

            def blk_stage(k, par):
                if not isinstance(k, int) or k + 1 < MAX_BLOCKS and k + 1 >= 0:
                    gate_exp(k + 1, (par + 1) % 2)
                if not isinstance(k, int) or 0 <= k < MAX_BLOCKS:
                    act_hi(k, par)
                if not isinstance(k, int) or k + 3 < MAX_BLOCKS:
                    rows_hi(k + 3, (par + 1) % 2)
                if not isinstance(k, int) or 0 <= k - 1:
                    rows_weighted(k - 1, (par + 1) % 2)

            for k in range(-3, 3):
                blk_stage(k, k % 2)
            pairs = (MAX_BLOCKS - 3 - 3) // 2
            with act.Fori(0, pairs) as j:
                blk_stage(2 * j + 3, 1)
                blk_stage(2 * j + 4, 0)
            for k in range(3 + 2 * pairs, MAX_BLOCKS + 1):
                blk_stage(k, k % 2)

        @block.vector
        def _(dve):
            chain = Chain(dve, setup_step, 0)

            def rsqrt(var, y, z):
                chain.link(dve.tensor_scalar(y.bitcast(I32), var.bitcast(I32), 1, None, ALU.logical_shift_right))
                chain.settle()
                chain.link(dve.tensor_scalar(y.bitcast(I32), y.bitcast(I32), -1.0, RSQRT_MAGIC, ALU.mult, ALU.add))
                chain.settle()
                for _ in range(3):
                    chain.link(dve.scalar_tensor_tensor(z, y, -0.5, y, ALU.mult, ALU.mult))
                    chain.settle()
                    chain.link(dve.tensor_tensor(z, z, var, ALU.mult))
                    chain.settle()
                    chain.link(dve.scalar_tensor_tensor(y, z, 1.5, y, ALU.add, ALU.mult))
                    chain.settle()

            def normalise_x(b):
                need(dve, x_sq, b, T)
                chain.link(dve.tensor_scalar(st_x[:, 1, :], st_x[:, 0, :], 1.0 / D, EPS, ALU.mult, ALU.add))
                chain.settle()
                rsqrt(st_x[:, 1, :], st_x[:, 2, :], st_x[:, 3, :])
                for t in range(T):
                    dve.tensor_scalar(xr_v[:, t, :], x_in[:, t, :], st_x[:, 2, t:t + 1], None,
                                      ALU.mult).then_inc(xr_ok.sem, 1)

            def modulate(b, c0=0):
                need(dve, xT_ps, b, 1)
                for c in range(C):
                    o = (c % 2) * N
                    dve.tensor_scalar(xn_v[:, c, :], ps_t[:, c // 2, o:o + N], a_mod[:, c, ds(b, 1)],
                                      s_mod[:, c, ds(b, 1)], ALU.mult, ALU.add).then_inc(xn_ok.sem, 1)

            def head_sums(b, u):
                t, kind = U_TILE[u], U_KIND[u]
                need(dve, qk_sq, b, u + 1)
                dve.tensor_reduce(st_s[:, t, kind * HEADS:(kind + 1) * HEADS],
                                  sq[:, u % 2, :].rearrange("p (h d) -> p h d", d=DH), AX.X, ALU.add).then_inc(hs_ok.sem, 1)

            def head_scales(b, t):
                need(dve, hs_ok, b, 2 * t + 2)
                chain.link(dve.tensor_scalar(st_q[:, t, 0, :], st_s[:, t, :], 1.0 / DH, EPS, ALU.mult, ALU.add))
                chain.settle()
                rsqrt(st_q[:, t, 0, :], st_q[:, t, 1, :], st_q[:, t, 2, :])

            def scale_heads(b, u):
                t, kind = U_TILE[u], U_KIND[u]
                v = qk_raw[:, u, :].rearrange("p (h d) -> p h d", d=DH)
                if kind == 0:
                    need(dve, gain_ok, b, t + 1)
                else:
                    need(dve, U_ev, b, u + 1)
                r = bcast(st_q[:, t, 1, kind * HEADS:(kind + 1) * HEADS], 2, DH)
                dve.tensor_tensor(v, v, r, ALU.mult).then_inc(qk_n.sem, 1)

            def parts_lo(b, s, u):
                need(dve, qk_hi, b, u + 1)
                t = U_TILE[u]
                cat = (q_cat, k_cat)[U_KIND[u]][s][:, t].rearrange("p h (r d) -> p h r d", d=DH)
                src = qk_raw[:, u, :].rearrange("p (h d) -> p h d", d=DH)
                dve.tensor_tensor(cat[:, :, 1 + U_KIND[u], :], src, cat[:, :, 0, :].bitcast(F32),
                                  ALU.subtract).then_inc(qk_lo.sem, 1)

            def stack_out(b, h):
                need(dve, T_ps, b, h + 1)
                need(dve, S_ps, b, h - 3)
                dve.tensor_copy(stk[0:PARTS, h % 4, :], ps_t[0:PARTS, h % 2, :]).then_inc(T_ed.sem, 1)

            def normalise_out(b, g):
                need(dve, V_ps, b, g + 1)
                need(dve, ohi_ok, b, g - 1)
                need(dve, olo_ok, b, g - 1)
                chain.link(dve.reciprocal(o_f[:, g % 2, :], ps_v[:, g % 2, N:2 * N]))
                chain.settle()
                dve.tensor_tensor(o_f[:, g % 2, :], ps_v[:, g % 2, 0:N], o_f[:, g % 2, :], ALU.mult).then_inc(nrm.sem, 1)

            def out_lo(b, g):
                need(dve, ohi_ok, b, g + 1)
                dve.tensor_tensor(o_lo[:, g, :], o_f[:, g % 2, :], o_hi[:, g, :].bitcast(F32),
                                  ALU.subtract).then_inc(olo_ok.sem, 1)

            def add_rows(b, t):
                need(dve, H_ev, b, t + 1)
                need(dve, xres_ld, b, 16)
                dve.tensor_tensor(xres[:, t, :], xres[:, t, :], h_sb[:, t, 0:D], ALU.add).then_inc(xh_ok.sem, 1)

            def picks(b):
                need(dve, H_ev, b, T)
                dve.sem_inc(dve_turn, 1)
                for t in range(T):
                    chain.link(dve.max(top_v[:, t, :], h_sb[:, t, D:WOC]))
                chain.settle()
                dve.sem_inc(dve_turn, 1)
                for t in range(T):
                    chain.link(dve.max_index(top_i[:, t, :], top_v[:, t, :], h_sb[:, t, D:WOC]))
                chain.settle()
                chain.link(dve.tensor_copy(top_f[:], top_i[:, :, 0:2]))
                dve.tensor_tensor(rt[:, 0, 0, :], top_v[:, :, 1], top_v[:, :, 0], ALU.subtract).then_inc(dif_ok.sem, 1)
                chain.settle()
                picks_f = top_f[:].rearrange("p t s -> p s t")
                chain.link(dve.tensor_tensor(oh[:], bcast(bcast(iota[:, 0:E], 1, T), 1, 2), bcast(picks_f, 3, E), ALU.is_equal))
                chain.link(dve.tensor_scalar(rt[:, 2], picks_f, float(BPE), None, ALU.mult))
                chain.settle()
                dve.tensor_tensor(mask[:], oh[:, 0], oh[:, 1], ALU.add).then_inc(mask_ok.sem, 1)

            def pick_weights(b):
                need(dve, ed_ok, b, 1)
                chain.link(dve.tensor_scalar(rt[:, 3, 0, :], rt[:, 1, 0, :], 1.0, None, ALU.add))
                chain.settle()
                chain.link(dve.reciprocal(rt[:, 4, 0, :], rt[:, 3, 0, :]))
                chain.settle()
                chain.link(dve.tensor_tensor(rt[:, 4, 1, :], rt[:, 1, 0, :], rt[:, 4, 0, :], ALU.mult))
                chain.settle()
                chain.link(dve.tensor_copy(w_hi_r[:], rt[:, 4]))
                chain.settle()
                chain.link(dve.tensor_tensor(rt[:, 5], rt[:, 4], w_hi_r[:].bitcast(F32), ALU.subtract))

            def slots(b):
                need(dve, Rp_ps, b, 1)
                need(dve, rank_ev, b - 1, 1)
                ps = ps_v[:, 1, 0:2 * E].rearrange("p (t e) -> p t e", t=T)
                chain.link(dve.tensor_tensor(ranks[:], ps, bcast(base[:], 1, T), ALU.add))
                chain.settle()
                dve.tensor_tensor(base[:], base[:], ps_v[:, 1, 2 * E:3 * E], ALU.add).then_inc(rank_ev.sem, 1)
                chain.link(dve.tensor_tensor(ohr[:, 0], oh[:, 0], ranks[:], ALU.mult))
                chain.link(dve.tensor_tensor(ohr[:, 1], oh[:, 1], ranks[:], ALU.mult))
                chain.settle()
                chain.link(dve.tensor_reduce(rt[:, 9], ohr[:], AX.X, ALU.add))
                chain.settle()
                chain.link(dve.tensor_copy(rt_i[:, 0], rt[:, 9]))
                chain.settle()
                chain.link(dve.tensor_scalar(rt_i[:, 1], rt_i[:, 0], P - 1, None, ALU.bitwise_and))
                chain.link(dve.tensor_scalar(rt_i[:, 2], rt_i[:, 0], 7, None, ALU.logical_shift_right))
                chain.settle()
                chain.link(dve.tensor_copy(rt[:, 6], rt_i[:, 1]))
                chain.link(dve.tensor_tensor(rt[:, 7], rt_i[:, 2], rt[:, 2], ALU.add))
                chain.settle()
                chain.link(dve.tensor_tensor(rt[:, 8], bcast(tok_c[:], 1, 2), rt[:, 6], ALU.subtract))
                chain.settle()
                chain.link(dve.tensor_scalar(tok_c[:], tok_c[:], float(N), None, ALU.add))

            def one_hots(b, i0):
                for i in range(i0, i0 + 2):
                    k, t = i // 2, i % 2
                    if i >= 2:
                        need(dve, Rt_ps, b, i - 1)
                    row, col = rt[:, 6, k, t:t + 1], rt[:, 7, k, t:t + 1]
                    dve.tensor_scalar(one_r[:, i % 2, :], iota[:], row, None, ALU.is_equal)
                    for m, val in enumerate((rt[:, 8, k, t:t + 1], rt[:, 4, k, t:t + 1], rt[:, 5, k, t:t + 1])):
                        v = w_hi_r[:, k, t:t + 1].bitcast(F32) if m == 1 else val
                        last = dve.tensor_scalar(one_c[:, i % 2, m, :], iota[:], col, v, ALU.is_equal, ALU.mult)
                    last.then_inc(hot_ok.sem, 1)

            def tables(b):
                need(dve, Rt_ps, b, 4)
                need(dve, tab_ev, b - 1, 1)
                t = tab[:].rearrange("p a n -> p (a n)")
                dve.tensor_tensor(t, t, ps_p[:, 0, 0:3 * P], ALU.add).then_inc(tab_ev.sem, 1)

            dve.sem_inc(rank_ev.sem, 1)
            dve.sem_inc(tab_ev.sem, 1)
            dve.memset(ones_r[:].bitcast(F32), 1.0).then_inc(consts, 1)
            dve.memset(xres[:, 0, :], 0.0).then_inc(zeroed, 1)
            dve.memset(tab[:, 1:3, :].rearrange("p a n -> p (a n)"), 0.0)
            dve.memset(base[:], 0.0)
            dve.wait_ge(consts, 5)
            dve.tensor_copy(ident_r[:], eye[:]).then_inc(consts, 1)
            dve.wait_ge(small_T, 1)
            dve.tensor_copy(embT[:].rearrange("p c b -> p (c b)"), ps_p[:, 0, 0:C * B])
            dve.tensor_copy(vecT[:], ps_p[:, 0, 64:76])
            dve.tensor_copy(wgT[:].rearrange("p c e -> p (c e)"), ps_p[:, 0, 128:128 + C * E]).then_inc(small_ok, 1)
            normalise_x(0)
            dve.wait_ge(ld_gains, 32)
            chain.link(dve.tensor_tensor(g_row[0:1, 2, :], g_row[0:1, 0, :], g_row[0:1, 1, :], ALU.mult))
            chain.settle()
            dve.tensor_scalar(g_row[0:1, 2, :], g_row[0:1, 2, :], float(DH) ** -0.5, None, ALU.mult).then_inc(gains_raw, 1)
            dve.wait_ge(ld_wout, 16)
            for c in range(C):
                last = dve.tensor_tensor(wpr[:, c, c * P:(c + 1) * P], wpr[:, c, c * P:(c + 1) * P], ident, ALU.add)
            last.then_inc(diag_ok, 1)
            dve.wait_ge(mod_ps, 1)
            dve.tensor_copy(mod_sb[0:B], ps_v[0:B]).then_inc(mod_rows, 1)
            dve.wait_ge(mod_T, 1)
            dve.wait_ge(small_ok, 1)
            for c in range(C):
                chain.link(dve.tensor_scalar(a_mod[:, c, :], ps_p[:, 0, c * B:(c + 1) * B], vecT[:, c:c + 1], 1.0, ALU.add, ALU.add))
                chain.link(dve.tensor_scalar(s_mod[:, c, :], ps_p[:, 0, (C + c) * B:(C + c + 1) * B], vecT[:, C + c:C + c + 1], None, ALU.add))
            chain.settle()
            for c in range(C):
                last = dve.tensor_scalar(a_mod[:, c, :], a_mod[:, c, :], vecT[:, 8 + c:9 + c], None, ALU.mult)
            last.then_inc(mod_ok, 1)
            dve.wait_ge(mod_ok, 1)
            modulate(0)
            dve.wait_ge(gains_ps, 1)
            dve.tensor_copy(gains[:], ps_s[:, 0, 0:DH]).then_inc(gains_ok, 1)
            dve.wait_ge(gains_ok, 1)
            chain.link(dve.tensor_reduce(g_max[:, 0:1], gains[:], AX.X, ALU.max, apply_absolute_value=True))
            chain.settle()
            chain.link(dve.tensor_scalar(g_max[:, 1:2], g_max[:, 0:1], -float(DH), SOFTMAX_SAFE, ALU.mult, ALU.add))
            chain.settle()
            chain.link(dve.tensor_scalar(shift[:], g_max[:, 1:2], 0.0, None, ALU.min))
            for c in range(1, C):
                dve.wait_ge(wqhi_ok, c + 1)
                dve.tensor_tensor(wq_lo[:, c, :], wq_raw[:, c, :], wq_hi[:, c, :].bitcast(F32), ALU.subtract).then_inc(wqlo_ok, 1)
            dve.wait_ge(wc_ps, 1)
            dve.tensor_copy(wc_sb[0:E, :], ps_v[0:E, 0, :]).then_inc(wc_rows, 1)
            for t in range(T):
                head_sums(0, 2 * t)
                head_sums(0, 2 * t + 1)
                head_scales(0, t)
                scale_heads(0, 2 * t)
                scale_heads(0, 2 * t + 1)
            normalise_x(1)
            dve.wait_ge(wc_T, 1)
            dve.tensor_copy(wpr[:, :, D:WOC], ps_v[:, 1, 0:C * E].rearrange("p (c e) -> p c e", c=C)).then_inc(wpr_ok, 1)
            for u in range(4):
                parts_lo(0, 0, u)
            modulate(1)
            dve.wait_ge(wohi_ok, 2)
            dve.tensor_tensor(wo_lo[:], wpr[:], wo_hi[:].bitcast(F32), ALU.subtract).then_inc(wolo_ok, 1)
            chain.begin(dve_step, DVE_STEPS)

            def step(b, s, nxt, ahead, routed):
                n, sn = b + 1, 1 - s
                chain.open(b)
                stack_out(b, 1)
                for g in range(G):
                    for j in range(4):
                        h, at = 4 * g + j, (g, j)
                        if h % 2 == 1 and h + 2 < HEADS:
                            stack_out(b, h + 2)
                        if routed:
                            if at == (0, 1):
                                picks(b - 1)
                            if at == (0, 3):
                                pick_weights(b - 1)
                            if at == (1, 0):
                                slots(b - 1)
                            if at == (1, 2):
                                one_hots(b - 1, 0)
                            if at == (2, 1):
                                one_hots(b - 1, 2)
                            if at == (2, 3):
                                tables(b - 1)
                        if ahead and at == (0, 3):
                            normalise_x(b + 2)
                        if at == (2, 0):
                            normalise_out(b, 0)
                        if at == (2, 2):
                            out_lo(b, 0)
                        if at == (3, 0):
                            normalise_out(b, 1)
                        if at == (3, 2):
                            out_lo(b, 1)
                        if nxt:
                            if at == (1, 1):
                                head_sums(n, 0)
                            if at == (2, 2):
                                head_sums(n, 1)
                                head_scales(n, 0)
                            if at == (3, 0):
                                scale_heads(n, 0)
                                scale_heads(n, 1)
                            if at == (3, 1):
                                head_sums(n, 2)
                            if at == (3, 2):
                                parts_lo(n, sn, 0)
                            if at == (3, 3):
                                parts_lo(n, sn, 1)
                normalise_out(b, 2)
                if nxt:
                    head_sums(n, 3)
                    head_scales(n, 1)
                out_lo(b, 2)
                normalise_out(b, 3)
                if nxt:
                    scale_heads(n, 2)
                    scale_heads(n, 3)
                out_lo(b, 3)
                if nxt:
                    parts_lo(n, sn, 2)
                    parts_lo(n, sn, 3)
                if ahead:
                    modulate(b + 2)
                add_rows(b, 0)
                add_rows(b, 1)
                chain.close()

            step(0, 0, True, True, False)
            with dve.Fori(0, (B - 2) // 2 - 1) as j:
                step(2 * j + 1, 1, True, True, True)
                step(2 * j + 2, 0, True, True, True)
            step(B - 3, 1, True, True, True)
            step(B - 2, 0, True, False, True)
            step(B - 1, 1, False, False, True)
            chain.open(B)
            picks(B - 1)
            pick_weights(B - 1)
            slots(B - 1)
            one_hots(B - 1, 0)
            one_hots(B - 1, 2)
            need(dve, rank_ev, B - 1, 1)
            L, S = chain.link, chain.settle
            nb, cb, gap = sched_f[:, 0, :], sched_f[:, 1, :], sched_f[:, 2, :]
            L(dve.tensor_scalar(n_i[:], base[:], float(P - 1), None, ALU.add)); S()
            L(dve.tensor_scalar(n_i[:], n_i[:], 7, None, ALU.logical_shift_right)); S()
            L(dve.tensor_copy(nb, n_i[:])); S()
            L(dve.tensor_copy(cb, nb))
            L(dve.tensor_scalar(gap, nb, -1.0, float(BPE), ALU.mult, ALU.add)); S()
            for k in (1, 2, 4):
                a, z = (sched_f[:, 1, :], sched_f[:, 3, :]) if k != 2 else (sched_f[:, 3, :], sched_f[:, 1, :])
                L(dve.tensor_tensor(z[:, k:], a[:, k:], a[:, 0:E - k], ALU.add))
                L(dve.tensor_copy(z[:, 0:k], a[:, 0:k])); S()
            cb = sched_f[:, 3, :]
            L(dve.tensor_tensor(sched_ge[:], bcast(iota[:, 0:MAX_BLOCKS], 2, E), bcast(cb, 1, MAX_BLOCKS), ALU.is_ge)); S()
            L(dve.tensor_reduce(sched_t[:, 0, :], sched_ge[:], AX.X, ALU.add)); S()
            L(dve.tensor_tensor(sched_ge[:], sched_ge[:], bcast(gap, 1, MAX_BLOCKS), ALU.mult))
            L(dve.tensor_scalar(sched_t[:, 1, :], sched_t[:, 0, :], float(E - 1), None, ALU.min)); S()
            L(dve.tensor_reduce(sched_t[:, 2, :], sched_ge[:], AX.X, ALU.add))
            L(dve.tensor_scalar(sched_t[:, 3, :], sched_t[:, 1, :], float(NSLOT), float(-NSLOT), ALU.is_ge, ALU.mult)); S()
            L(dve.tensor_tensor(sched_t[:, 2, :], sched_t[:, 2, :], iota[:, 0:MAX_BLOCKS], ALU.add))
            L(dve.tensor_tensor(sched[:, 1, :], sched_t[:, 1, :], sched_t[:, 3, :], ALU.add))
            L(dve.tensor_scalar(sched[:, 2, :], sched_t[:, 1, :], 1.0, 16.0, ALU.add, ALU.mult)); S()
            L(dve.tensor_scalar(sched[:, 0, :], sched_t[:, 2, :], float(P), None, ALU.min))
            dve.tensor_scalar(free_at[:], cb, 1.0, None, ALU.add).then_inc(sched_ok, 1)
            tables(B - 1)
            need(dve, tab_ev, B - 1, 1)
            L(dve.tensor_copy(tab_id[:, 0:P], tab[:, 0, :]))
            L(dve.tensor_tensor(tab_w[:, 0:P], tab[:, 1, :], tab[:, 2, :], ALU.add)); S()
            L(dve.tensor_copy(tab_id[:, P:P + 1], spare_row[:]))
            dve.memset(tab_w[:, P:P + 1], 0.0).then_inc(tabs_ok, 1)
            assert chain.n <= DVE_STEPS

            blkc = Chain(dve, blk_step, 3)

            def swiglu(k, s):
                need(dve, e_ok, k, 1)
                need(dve, gT_ps, k - 2, 1)
                blkc.open(k)
                blkc.link(dve.tensor_scalar(sg[:, s, :], sg[:, s, :], 1.0, None, ALU.add)); blkc.settle()
                blkc.link(dve.reciprocal(sg[:, s, :], sg[:, s, :])); blkc.settle()
                blkc.link(dve.tensor_tensor(sg[:, s, :], ps_p[:, s, 0:H], sg[:, s, :], ALU.mult)); blkc.settle()
                dve.tensor_tensor(gu[:, s, :], ps_p[:, s, H:2 * H], sg[:, s, :], ALU.mult).then_inc(gu_ok.sem, 1)

            def act_lo(k, s):
                need(dve, gh_ok, k, 1)
                dve.tensor_tensor(gu_lo[:, s, :], ps_v[:, s, 0:H], gu_hi[:, s, :].bitcast(F32), ALU.subtract).then_inc(gl_ok.sem, 1)

            def rows_lo(k, s):
                need(dve, xgh_ok, k, 1)
                dve.tensor_tensor(xg_lo[:, s, :], ps_t[:, s, :], xg_hi[:, s, :].bitcast(F32), ALU.subtract).then_inc(xgl_ok.sem, 1)

            def blk_stage(k, par):
                if not isinstance(k, int) or k + 1 < MAX_BLOCKS and k + 1 >= 0:
                    swiglu(k + 1, (par + 1) % 2)
                if not isinstance(k, int) or 0 <= k < MAX_BLOCKS:
                    act_lo(k, par)
                if not isinstance(k, int) or k + 3 < MAX_BLOCKS:
                    rows_lo(k + 3, (par + 1) % 2)

            for k in range(-3, 3):
                blk_stage(k, k % 2)
            pairs = (MAX_BLOCKS - 3 - 3) // 2
            with dve.Fori(0, pairs) as j:
                blk_stage(2 * j + 3, 1)
                blk_stage(2 * j + 4, 0)
            for k in range(3 + 2 * pairs, MAX_BLOCKS + 1):
                blk_stage(k, k % 2)

        @block.gpsimd
        def _(pool):
            def gain_unit(b, t):
                u = 2 * t
                need(pool, U_ev, b, u + 1)
                q = qk_raw[:, u, :].rearrange("p (h d) -> p h d", d=DH)
                pool.tensor_tensor(q, q, bcast(gains[:], 1, HEADS), ALU.mult).then_inc(gain_ok.sem, 1)

            def x_lo_part(b):
                need(pool, xhi_ok, b, 1)
                need(pool, U_ps, b - 1, 6)
                pool.tensor_tensor(x_lo[:].rearrange("p c n -> p (c n)"), xn[:],
                                   x_hi[:].rearrange("p c n -> p (c n)").bitcast(F32), ALU.subtract).then_inc(xlo_ok.sem, 1)

            def split_lo(e, p):
                s = p % 2
                need(pool, ehi_ok, e, p + 1)
                pool.tensor_tensor(e_raw[:, s, :], e_raw[:, s, :], e_hi[:, s, :].bitcast(F32), ALU.subtract).then_inc(elo_ok.sem, 1)

            pool.memset(tri[:].bitcast(F32), 1.0).then_inc(pool_turn, 1)
            pool.memset(eye[:], 0.0).then_inc(pool_turn, 1)
            pool.wait_ge(pool_turn, 2)
            pool.affine_select(out=eye[:], in_=eye[:], compare_op=ALU.not_equal, fill=1.0, base=0,
                               pattern=[[-1, P]], channel_multiplier=1).then_inc(consts, 1)
            pool.affine_select(out=tri[:], in_=tri[:].bitcast(F32), compare_op=ALU.is_gt, fill=0.0, base=0,
                               pattern=[[1, P]], channel_multiplier=-1).then_inc(consts, 1)
            pool.iota(iota[:], pattern=[[1, P]], base=0, channel_multiplier=0,
                      allow_small_or_imprecise_dtypes=True)
            pool.iota(spare_row[:], pattern=[[0, 1]], base=TOK, channel_multiplier=1,
                      allow_small_or_imprecise_dtypes=True).then_inc(consts, 1)
            pool.iota(tab[:, 0, :], pattern=[[0, P]], base=TOK, channel_multiplier=1,
                      allow_small_or_imprecise_dtypes=True)
            pool.iota(tok_c[:], pattern=[[P, T]], base=-TOK, channel_multiplier=1,
                      allow_small_or_imprecise_dtypes=True).then_inc(consts, 1)
            pool.wait_ge(wqhi_ok, 1)
            pool.tensor_tensor(wq_lo[:, 0, :], wq_raw[:, 0, :], wq_hi[:, 0, :].bitcast(F32), ALU.subtract).then_inc(wqlo0_ok, 1)
            x_lo_part(0)
            pool.wait_ge(gains_ok, 1)
            gain_unit(0, 0)
            gain_unit(0, 1)
            x_lo_part(1)

            def step(b, nxt, ahead):
                n = b + 1
                split_lo(b, 0)
                if nxt:
                    gain_unit(n, 0)
                for p in range(1, 4):
                    split_lo(b, p)
                if nxt:
                    gain_unit(n, 1)
                for p in range(4, 6):
                    split_lo(b, p)
                if ahead:
                    x_lo_part(b + 2)

            step(0, True, True)
            with pool.Fori(1, B - 2) as b:
                step(b, True, True)
            step(B - 2, True, False)
            step(B - 1, False, False)

            def column(k):
                return pool.value_load(sched[0:1, 0, ds(k, 1)], min_val=0, max_val=P)

            def gather(k, s):
                col = column(k)
                need(pool, xg_ld[s], k - 2, 16 - 8 * s)
                pool.sem_inc(pool_turn, 1)
                pool.tensor_copy(g_idx[:, s, :], tab_id[:, ds(col, 1)]).then_inc(col_ok.sem, 1)
                need(pool, xgT_ps, k - 2, 1)
                pool.sem_inc(pool_turn, 1)
                need(pool, col_ok, k, 1)
                pool.sem_inc(pool_turn, 1)
                pool.indirect_dma_start(out=xg[:, s, :], out_offset=None, in_=h_rows,
                                        in_offset=bass.IndirectOffsetOnAxis(ap=g_idx[:, s, :].bitcast(U32), axis=0)).then_inc(xg_ld[s].sem, 16)

            def pick(k, s):
                col = column(k)
                need(pool, y_ok, k - 2, 1)
                pool.sem_inc(pool_turn, 1)
                need(pool, acc_st, k - 2, 16)
                pool.sem_inc(pool_turn, 1)
                pool.tensor_copy(w_sel[:, s, :], tab_w[:, ds(col, 1)]).then_inc(wsel_ok.sem, 1)
                pool.tensor_copy(s_idx[:, s, :], tab_id[:, ds(col, 1)]).then_inc(wsel_ok.sem, 1)

            def scatter(k, s):
                need(pool, acc_st, k - 1, 16)
                pool.sem_inc(pool_turn, 1)
                need(pool, wsel_ok, k, 2)
                pool.sem_inc(pool_turn, 1)
                need(pool, y_ok, k, 1)
                pool.sem_inc(pool_turn, 1)
                pool.indirect_dma_start(out=out, out_offset=bass.IndirectOffsetOnAxis(ap=s_idx[:, s, :].bitcast(U32), axis=0),
                                        in_=y_sb[:, s, :], in_offset=None, compute_op=ALU.add).then_inc(acc_st.sem, 16)

            pool.wait_ge(spare_st, 32)
            for t in range(T):
                need(pool, row_st[t], B - 1, 32)
            pool.wait_ge(sched_ok, 1)
            pool.wait_ge(tabs_ok, 1)

            def blk_stage(k, par):
                if not isinstance(k, int) or k + 4 < MAX_BLOCKS:
                    gather(k + 4, par)
                if not isinstance(k, int) or 0 <= k < MAX_BLOCKS:
                    pick(k, par)
                if not isinstance(k, int) or 0 <= k - 1:
                    scatter(k - 1, (par + 1) % 2)

            for k in range(-4, 3):
                blk_stage(k, k % 2)
            pairs = (MAX_BLOCKS - 3 - 4) // 2
            with pool.Fori(0, pairs) as j:
                blk_stage(2 * j + 3, 1)
                blk_stage(2 * j + 4, 0)
            for k in range(3 + 2 * pairs, MAX_BLOCKS + 1):
                blk_stage(k, k % 2)


_INS = ['x', 'cond_2048', 'L0_cond_W_emb', 'L0_cond_b_emb', 'L0_cond_g_norm', 'L0_cond_W_qkv', 'L0_cond_g_q',
        'L0_cond_g_k', 'L0_cond_W_out', 'L0_ffn_W_gate', 'L0_ffn_w_gate_proj', 'L0_ffn_w_up_proj', 'L0_ffn_w_down_proj']


def kernel(**inputs):
    import numpy as np
    import concourse.bacc as bacc
    from concourse.bass_utils import run_bass_kernel_spmd

    nc = bacc.Bacc("TRN2", target_bir_lowering=False, num_devices=1)
    arrays, args = {}, []
    for name in _INS:
        a = np.ascontiguousarray(inputs[name])
        arrays[f"in_{name}"] = a
        args.append(nc.dram_tensor(f"in_{name}", a.shape, mybir.dt.from_np(a.dtype), kind="ExternalInput").ap())
    b, n, d = inputs["x"].shape
    out = nc.dram_tensor("out_rows", (b * n + P, d), F32, kind="ExternalOutput").ap()
    adaln_moe_kernel(nc, *args, out)
    r = run_bass_kernel_spmd(nc, [arrays], core_ids=[0])
    return r.results[0]["out_rows"][:b * n].reshape(b, n, d)
```
